# Optimizing a Trainium2 kernel written in Bass

```python
import numpy as np
import jax
import jax.numpy as jnp

def _softmax(x, axis=-1):
    return jax.nn.softmax(x, axis=axis)

def _gelu(x):
    return jax.nn.gelu(x, approximate=True)

def _silu(x):
    return jax.nn.silu(x)

def _sigmoid(x):
    return jax.nn.sigmoid(x)

def _layernorm(x, axis=-1, eps=1e-05):
    m = jnp.mean(x, axis=axis, keepdims=True)
    v = jnp.var(x, axis=axis, keepdims=True)
    return (x - m) / jnp.sqrt(v + eps)

def _scatter_add(tgt, idx, src, axis=0):
    return tgt.at[idx].add(src)

def _segment_sum(src, seg, n):
    return jax.ops.segment_sum(src, seg, n)
kernel_name = 'mk_gnn_preln_d2_gnn_r32_c69fe7'

def setup_inputs(seed: int=0):
    np.random.seed(seed)
    _w = jnp.asarray

    def _rec_inputs():
        import jax
        import jax.numpy as jnp
        _gk = jax.random.key(seed)
        x = -0.000202 + 1 * jax.random.normal(jax.random.fold_in(_gk, 1), (3125, 64), jnp.float32)
        _s = jax.random.randint(jax.random.fold_in(_gk, 2), (50000,), 0, 3125, jnp.int32)
        _d = jax.random.randint(jax.random.fold_in(_gk, 3), (50000,), 0, 3125, jnp.int32)
        _loop = jnp.arange(3125, dtype=jnp.int32)
        src = jnp.concatenate([_s, _d, _loop])
        dst = jnp.concatenate([_d, _s, _loop])
        _o = jnp.argsort(dst, stable=True)
        src = src[_o]
        dst = dst[_o]
        edge_weight = jax.random.uniform(jax.random.fold_in(_gk, 13), (103125,), jnp.float32, 0.0, 0.2)
        return (x, src, dst, edge_weight)
    x, src, dst, edge_weight = _rec_inputs()

    def _L0_gnn_setup():
        import jax, jax.numpy as jnp
        import numpy as np
        N_NODES = 3125
        N_EDGES = 50000
        C_IN = 64
        C_OUT = 64
        BN_EPS = 1e-05
        key = jax.random.key(seed)
        k1, k2, k3, k4, k5 = jax.random.split(key, 5)
        x_bk_c = jax.random.normal(k1, (N_NODES, C_IN), dtype=jnp.float32)
        edge_index_batched = jax.random.randint(k2, (2, N_EDGES), 0, N_NODES, dtype=jnp.int64)
        W = jax.random.normal(k3, (C_OUT, 2 * C_IN), dtype=jnp.float32) / np.sqrt(2 * C_IN)
        bn_gamma = jnp.ones((C_OUT,), dtype=jnp.float32)
        bn_beta = jnp.zeros((C_OUT,), dtype=jnp.float32)
        bn_mean = 0.1 * jax.random.normal(k4, (C_OUT,), dtype=jnp.float32)
        bn_var = jnp.abs(1.0 + 0.1 * jax.random.normal(k5, (C_OUT,), dtype=jnp.float32))
        return {'x_bk_c': x_bk_c, 'edge_index_batched': edge_index_batched, 'W': W, 'bn_gamma': bn_gamma, 'bn_beta': bn_beta, 'bn_mean': bn_mean, 'bn_var': bn_var}
    _L0_gnn_all = _L0_gnn_setup()
    _L0_gnn_in = {k: v for k, v in _L0_gnn_all.items() if k in ('W', 'bn_gamma', 'bn_beta', 'bn_mean', 'bn_var')}
    del _L0_gnn_all

    def _L1_gnn_setup():
        import jax, jax.numpy as jnp
        import numpy as np
        N = 3125
        D = 64
        E = 31250
        L = 10
        ALPHA = 0.3
        EPS = 1e-08
        key = jax.random.key(seed)
        k1, k2, k3, k4 = jax.random.split(key, 4)
        edge_src = jax.random.randint(k1, (E,), 0, N)
        edge_dst = jax.random.randint(k2, (E,), 0, N)
        edge_vals = jax.random.uniform(k3, (E,), dtype=jnp.float32) * 0.2
        X = jax.random.normal(k4, (N, D), dtype=jnp.float32)
        l_idx = jnp.arange(L + 1, dtype=jnp.float32)
        manifold_weights = ALPHA * (1.0 - ALPHA) ** (l_idx * 1.5)
        return {'X': X, 'edge_vals': edge_vals, 'manifold_weights': manifold_weights, 'edge_src': edge_src, 'edge_dst': edge_dst}
    _L1_gnn_all = _L1_gnn_setup()
    _L1_gnn_in = {k: v for k, v in _L1_gnn_all.items() if k in ('manifold_weights',)}
    del _L1_gnn_all
    return {'x': x, 'src': src, 'dst': dst, 'edge_weight': edge_weight, 'L0_gnn_W': _L0_gnn_in['W'], 'L0_gnn_bn_gamma': _L0_gnn_in['bn_gamma'], 'L0_gnn_bn_beta': _L0_gnn_in['bn_beta'], 'L0_gnn_bn_mean': _L0_gnn_in['bn_mean'], 'L0_gnn_bn_var': _L0_gnn_in['bn_var'], 'L1_gnn_manifold_weights': _L1_gnn_in['manifold_weights']}

def reference(x, src, dst, edge_weight, L0_gnn_W, L0_gnn_bn_gamma, L0_gnn_bn_beta, L0_gnn_bn_mean, L0_gnn_bn_var, L1_gnn_manifold_weights):
    import jax
    import jax.numpy as jnp

    def _L0_gnn_ref(x_bk_c, edge_index_batched, W, bn_gamma, bn_beta, bn_mean, bn_var):
        import jax, jax.numpy as jnp
        import numpy as np
        N_NODES = 3125
        N_EDGES = 50000
        C_IN = 64
        C_OUT = 64
        BN_EPS = 1e-05
        row = edge_index_batched[0]
        col = edge_index_batched[1]
        x_i = x_bk_c[row]
        x_j = x_bk_c[col]
        e = jnp.concatenate((x_i, x_j - x_i), axis=1)
        h = jnp.einsum('ec,oc->eo', e, W)
        inv = bn_gamma * jax.lax.rsqrt(bn_var + BN_EPS)
        h = h * inv + (bn_beta - bn_mean * inv)
        h = h * jax.nn.sigmoid(h)
        x_out = jax.ops.segment_sum(h, row, num_segments=x_bk_c.shape[0])
        return x_out

    def _L1_gnn_ref(X, edge_vals, manifold_weights, edge_src, edge_dst):
        import jax, jax.numpy as jnp
        import numpy as np
        N = 3125
        D = 64
        E = 31250
        L = 10
        ALPHA = 0.3
        EPS = 1e-08
        n = X.shape[0]

        def spmm(H):
            return jax.ops.segment_sum(edge_vals[:, None] * H[edge_src], edge_dst, num_segments=n)
        H = X
        Z = manifold_weights[0] * H
        for l in range(1, L + 1):
            H = spmm(H)
            Hn = jnp.linalg.norm(H, axis=1, keepdims=True)
            H = H / (Hn + EPS) * jnp.tanh(Hn + EPS)
            Z = Z + manifold_weights[l] * H
        return Z
    edge_index = jnp.stack([src, dst])
    h = jnp.maximum(_layernorm(x, axis=-1), 0.0)
    x = x + _L0_gnn_ref(h, edge_index, L0_gnn_W, L0_gnn_bn_gamma, L0_gnn_bn_beta, L0_gnn_bn_mean, L0_gnn_bn_var)
    h = jnp.maximum(_layernorm(x, axis=-1), 0.0)
    x = x + _L1_gnn_ref(h, edge_weight, L1_gnn_manifold_weights, src, dst)
    return x

_drawn_inputs = setup_inputs


def setup_inputs(seed=0):
    import zlib

    import numpy as np

    out = dict(_drawn_inputs(seed))
    spreads = {'L0_gnn_bn_gamma': (1.0, 0.2), 'L0_gnn_bn_beta': (0.0, 0.1)}
    factors = {'edge_weight': 8.0, 'L1_gnn_manifold_weights': 4.572}
    for name, (base, spread) in spreads.items():
        noise = np.random.default_rng([zlib.crc32(name.encode()), seed]).standard_normal(out[name].shape)
        drawn = base * np.exp(spread * noise) if base else spread * noise
        out[name] = jnp.asarray(drawn.astype(out[name].dtype))
    for name, factor in factors.items():
        out[name] = (out[name] * factor).astype(out[name].dtype)
    return out
```

```python
from contextlib import ExitStack

import concourse.bass as bass
from concourse import mybir

F32 = mybir.dt.float32
F16 = mybir.dt.float16
I32 = mybir.dt.int32
I16 = mybir.dt.int16
ALU = mybir.AluOpType
ACT = mybir.ActivationFunctionType
AX = mybir.AxisListType

N = 3125
C = 64
P = 125
NJ = N // P
E = 103125
T = E // P
G = 11
SLOTS = 3
NG = T // G
BODY = NG // SLOTS
OH = 3
CHUNK = 500
BPC = CHUNK // P
CHUNKS = [(c * CHUNK, min(CHUNK, N - c * CHUNK)) for c in range(-(-N // CHUNK))]
NC = len(CHUNKS)
LAYERS = 10
UJ = 5
NQ = NJ // UJ
RESIDENT = (1, 4)
STREAMED = (NC - 1) * (NQ - len(RESIDENT))
RING = 3
LN_EPS = 1e-5
BN_EPS = 1e-5
NORM_EPS = 1e-8
W_UP = 512.0
RSQRT_MAGIC = float(0x5F3759DF)
A_HI = 2.0 ** -11
H_UP = 4096.0
UNSCALE = 1.0 / (W_UP * A_HI * H_UP)


def gnn_kernel(nc, x_d, src_d, dst_d, ew_d, w_d, gamma_d, beta_d, mean_d, var_d, mix_d, out_d):
    p_d = nc.dram_tensor("p_rows", (N, C), F32, kind="Internal").ap()
    q_d = nc.dram_tensor("q_rows", (N, C), F32, kind="Internal").ap()
    key_d = nc.dram_tensor("key_rows", (T, P), F32, kind="Internal").ap()
    adj_d = nc.dram_tensor("adjacency", (N * N + P, 1), F32, kind="Internal").ap()
    adj_rows = adj_d[0:N * N, :].rearrange("(j p d) o -> p j (d o)", p=P, d=N)
    split_d = nc.dram_tensor("split_units", (STREAMED, P, UJ * 2 * CHUNK), F16, kind="Internal").ap()

    ctx = ExitStack()
    with ctx:
        def sb(name, shape, dt):
            return ctx.enter_context(nc.sbuf_tensor(name, shape, dt))

        def sem(name):
            return ctx.enter_context(nc.semaphore(name))

        ps = [ctx.enter_context(nc.psum_tensor(f"bank{b}", [128, 512], F32)) for b in range(8)]

        z_acc = sb("z_acc", [P, NJ, C], F32)
        mix = sb("mix", [P, LAYERS + 1], F32)
        fold = sb("fold", [128, C], F32)
        hh_all = sb("hh_all", [P, 4, NJ, 2 * C], F16)
        hh = [[hh_all[:, 2 * a + s] for s in range(2)] for a in range(2)]
        stage0 = sb("stage0", [P, UJ * CHUNK], F32)
        UNIT = UJ * 2 * CHUNK
        LAST = NJ * 2 * P
        n_res = (NC - 1) * len(RESIDENT)
        ARENA = (n_res + RING) * UNIT + LAST
        arena = sb("arena", [P, ARENA], F16)
        res = [arena[:, k * UNIT:(k + 1) * UNIT].rearrange("p (j h d) -> p j h d", j=UJ, h=2) for k in range(n_res)]
        last_adj = arena[:, n_res * UNIT:n_res * UNIT + LAST].rearrange("p (j h d) -> p j h d", j=NJ, h=2)
        ring = [arena[:, n_res * UNIT + LAST + k * UNIT:n_res * UNIT + LAST + (k + 1) * UNIT]
                .rearrange("p (j h d) -> p j h d", j=UJ, h=2) for k in range(RING)]
        stage = [stage0[:, :], arena[:, ARENA - UNIT:ARENA].bitcast(F32)]
        at = [0]

        def carve(shape, dt):
            n = 1
            for s in shape:
                n *= s
            halves = n if dt in (F16, I16) else 2 * n
            at[0] += at[0] % 2
            v = arena[:, at[0]:at[0] + halves]
            at[0] += halves
            assert at[0] <= ARENA
            v = v if dt == F16 else v.bitcast(dt)
            if len(shape) == 2:
                v = v.rearrange("p (a b) -> p a b", b=shape[1])
            return v

        src_i = carve([T], I32)
        dst_i = carve([T], I32)
        w_up = carve([T], F32)
        src_f = carve([T], F32)
        key_f = carve([T], F32)
        to_spare = carve([T], F32)
        iota16 = carve([N + 1], I16)
        onehot = [carve([N + 1], F16) for _ in range(OH)]
        ident = carve([P], F32)
        before = carve([P], F32)
        iota_sq = carve([P], I32)
        spare_i = carve([1], I32)
        keyrow = [carve([G, P], F32) for _ in range(SLOTS)]
        equal = carve([G, P], F32)
        repeat = [carve([G, P], F32) for _ in range(SLOTS)]
        count = carve([G], F32)
        shift = carve([G], F32)
        src_x = [carve([G], I32) for _ in range(SLOTS)]
        dst_x = [carve([G], I32) for _ in range(SLOTS)]
        adj_x = [carve([G], I32) for _ in range(SLOTS)]
        src_c = [carve([G], F32) for _ in range(SLOTS)]
        w_c = [carve([G], F32) for _ in range(SLOTS)]
        w_sum = [carve([G], F32) for _ in range(SLOTS)]
        gathers_at = at[0]
        p_g = [carve([G, C], F32) for _ in range(SLOTS)]
        q_g = [carve([G, C], F32) for _ in range(SLOTS)]
        norm_s = arena[:, gathers_at:gathers_at + 2 * NJ * C].bitcast(F32).rearrange("p (j c) -> p j c", c=C)
        assert at[0] >= gathers_at + 2 * NJ * C
        messages_at = at[0]
        pre = [carve([G, C], F32) for _ in range(SLOTS)]
        msg = [carve([G, C], F32) for _ in range(SLOTS)]
        h0t = arena[:, messages_at:messages_at + 2 * N].bitcast(F32)
        assert at[0] >= messages_at + 2 * N
        msg16 = [carve([G, 2 * C], F16) for _ in range(SLOTS)]
        key_t = carve([G, P], F32)
        zeros = carve([N], F32)
        zeros16 = carve([128 + CHUNK], F16)
        norm_c = carve([NJ, C], F32)
        pq = hh_all[:, 0:2].rearrange("p a j c -> p (a j c)").bitcast(F32).rearrange("p (j c) -> p j c", c=2 * C)
        w_nat = carve([2 * C], F32)
        w_t = carve([2 * C], F32)
        w_fold = carve([2 * C], F32)
        bn = carve([4, C], F32)
        inv = carve([C], F32)
        bias = carve([C], F32)
        halves_sb = [sb(f"halves_sb{k}", [128, CHUNK], F32) for k in range(2)]
        stat = [sb(f"stat{k}", [P, NJ], F32) for k in range(4)]
        square = sb("square", [P, BPC * C], F32)
        h_new = sb("h_new", [P, BPC * C], F32)
        n_sq = [sb(f"n_sq{k}", [P, BPC], F32) for k in range(2)]
        n_eps = [sb(f"n_eps{k}", [P, BPC], F32) for k in range(2)]
        n_tanh = [sb(f"n_tanh{k}", [P, BPC], F32) for k in range(2)]
        factor = [sb(f"factor{k}", [P, BPC], F32) for k in range(2)]
        iota_fold = halves_sb[1][:, 0:C].bitcast(I32)
        fold_b = halves_sb[0][:, 0:C]

        edges_loaded, x_loaded, bn_loaded, mix_loaded, w_loaded = (
            sem(n) for n in ("edges_loaded", "x_loaded", "bn_loaded", "mix_loaded", "w_loaded"))
        iotas_ready, ident_ready, zeros_ready = sem("iotas_ready"), sem("ident_ready"), sem("zeros_ready")
        zero_filled = sem("zero_filled")
        key_ready, key_turned, key_t_copied, key_stored = (
            sem("key_ready"), sem("key_turned"), sem("key_t_copied"), sem("key_stored"))
        h0_ready, h0_turned, h0t_copied = sem("h0_ready"), sem("h0_turned"), sem("h0t_copied")
        w_turned, w_folded, pq_made, pq_ready, pq_stored = (
            sem("w_turned"), sem("w_folded"), sem("pq_made"), sem("pq_ready"), sem("pq_stored"))
        dve_step = sem("dve_step")
        keyrow_loaded = [sem(f"keyrow_loaded{s}") for s in range(SLOTS)]
        gathered = [sem(f"gathered{s}") for s in range(SLOTS)]
        keyrow_free, tiles_begun, groups_begun, repeat_ready, repeat_summed, prep_ready = (
            sem("keyrow_free"), sem("tiles_begun"), sem("groups_begun"), sem("repeat_ready"), sem("repeat_summed"), sem("prep_ready"))
        scattered = sem("scattered")
        pre_ready, msg_hi_ready, msg_ready = sem("pre_ready"), sem("msg_hi_ready"), sem("msg_ready")
        msg_done = sem("msg_done")
        pq_copied = sem("pq_copied")
        onehot_ready, onehot_free = sem("onehot_ready"), sem("onehot_free")
        out0_ready, out0_copied, out0_turned, out0_added = (
            sem("out0_ready"), sem("out0_copied"), sem("out0_turned"), sem("out0_added"))
        h1_ready = sem("h1_ready")
        adj_loaded = [sem(f"adj_loaded{k}") for k in range(2)]
        adj_hi_ready, adj_split, stage_free = sem("adj_hi_ready"), sem("adj_split"), sem("stage_free")
        unit_stored = sem("unit_stored")
        streamed = [sem(f"streamed{k}") for k in range(RING)]
        unit_used = sem("unit_used")
        product_ready, bank_free, turned, squared, eps_ready, tanh_ready, new_ready, hi_ready, hh_ready = (
            sem(n) for n in ("product_ready", "bank_free", "turned", "squared", "eps_ready", "tanh_ready",
                             "new_ready", "hi_ready", "hh_ready"))
        out_stored = sem("out_stored")

        block = ctx.enter_context(nc.Block())

        units = [(c, q) for c in range(NC - 1) for q in range(NQ)]
        streamed_of = {}
        resident_of = {}
        for c, q in units:
            if q in RESIDENT:
                resident_of[c, q] = len(resident_of)
            else:
                streamed_of[c, q] = len(streamed_of)

        SPLITS = [(c, q, UJ * q, UJ) for c, q in units] + [(NC - 1, 0, 0, 20), (NC - 1, 1, 20, 5)]

        def split_out(c, q):
            if c == NC - 1:
                return last_adj[:, 20 * q:20 + 5 * q]
            return res[resident_of[c, q]] if (c, q) in resident_of else ring[streamed_of[c, q] % 2]

        @block.sync
        def _(sp):
            for dram, tile in ((src_d, src_i), (dst_d, dst_i), (ew_d, w_up)):
                sp.dma_start(tile, dram.rearrange("(p t) -> p t", t=T)).then_inc(edges_loaded, 16)
            sp.dma_start(z_acc[:], x_d.rearrange("(j p) c -> p j c", p=P)).then_inc(x_loaded, 16)
            sp.dma_start(w_nat[0:C, :], w_d).then_inc(w_loaded, 16)
            for k, dram in enumerate((gamma_d, beta_d, mean_d, var_d)):
                sp.dma_start(bn[:, k, :], dram.partition_broadcast(P)).then_inc(bn_loaded, 16)
            sp.dma_start(mix[:], mix_d.partition_broadcast(P)).then_inc(mix_loaded, 16)
            sp.wait_ge(key_t_copied, 3)
            sp.dma_start(key_d.rearrange("(a q) p -> q a p", q=T // G), key_t[0:T // G]).then_inc(key_stored, 16)
            sp.wait_ge(pq_ready, 1)
            sp.dma_start(p_d.rearrange("(j p) c -> p j c", p=P), pq[:, :, 0:C]).then_inc(pq_stored, 16)
            sp.dma_start(q_d.rearrange("(j p) c -> p j c", p=P), pq[:, :, C:2 * C]).then_inc(pq_stored, 16)
            sp.wait_ge(zeros_ready, 1)
            for j in range(NJ):
                sp.dma_start(adj_rows[:, j, :], zeros).then_inc(zero_filled, 16)
            sp.wait_ge(key_stored, 16)
            key_flat = key_d.rearrange("t p -> (t p)")
            with sp.Fori(0, BODY) as i:
                for s in range(SLOTS):
                    sp.wait_ge(keyrow_free, i * SLOTS + (s + 1))
                    sp.dma_start(keyrow[s].rearrange("p a b -> p (a b)"),
                                 key_flat[bass.ds((i * SLOTS + s) * (G * P), G * P)].partition_broadcast(P)
                                 ).then_inc(keyrow_loaded[s], 16)
            sp.wait_ge(scattered, 16 * T + 16)
            sp.wait_ge(hh_ready, NC)
            for k, (c, q, j0, nj) in enumerate(SPLITS):
                d0, nd = CHUNKS[c]
                if k >= 2:
                    sp.wait_ge(stage_free, k - 1)
                sp.dma_start(stage[k % 2][:, 0:nj * nd].rearrange("p (j d) -> p j d", d=nd),
                             adj_rows[:, j0:j0 + nj, d0:d0 + nd]).then_inc(adj_loaded[k % 2], 16)
            sp.wait_ge(unit_stored, 16 * STREAMED)
            sp.wait_ge(stage_free, len(SPLITS))
            with sp.Fori(0, LAYERS // 2) as i:
                for v in range(2 * STREAMED):
                    sp.wait_ge(unit_used, i * (2 * STREAMED) + (v + 1))
                    sp.dma_start(ring[v % RING].rearrange("p j h d -> p (j h d)"),
                                 split_d[v % STREAMED]).then_inc(streamed[v % RING], 16)
            sp.wait_ge(hh_ready, NC * (LAYERS + 1))
            sp.dma_start(out_d.rearrange("(j p) c -> p j c", p=P), z_acc[:]).then_inc(out_stored, 16)
            sp.wait_ge(out_stored, 16)

        @block.gpsimd
        def _(pool):
            nc.gpsimd.iota(iota16, pattern=[[1, N + 1]], base=0, channel_multiplier=0).then_inc(iotas_ready, 1)
            nc.gpsimd.iota(iota_sq, pattern=[[1, P]], base=0, channel_multiplier=-1).then_inc(iotas_ready, 1)
            nc.gpsimd.iota(spare_i, pattern=[[1, 1]], base=N * N, channel_multiplier=1).then_inc(iotas_ready, 1)
            nc.gpsimd.iota(iota_fold, pattern=[[1, C]], base=0, channel_multiplier=-1).then_inc(iotas_ready, 1)
            pool.sem_inc(tiles_begun, 2 * G)
            pool.wait_ge(zeros_ready, 1)
            nc.gpsimd.dma_start(adj_d[N * N:N * N + P, :], zeros[:, 0:1]).then_inc(scattered, 16)
            pool.wait_ge(pq_stored, 32)
            pool.wait_ge(zero_filled, 16 * NJ)

            def group(i, s):
                pool.wait_ge(prep_ready, i * SLOTS + (s + 1))
                pool.sem_inc(groups_begun, 1)
                for k in range(G):
                    t = i * (SLOTS * G) + (s * G + k)
                    nc.gpsimd.indirect_dma_start(
                        out=p_g[s][:, k, :], out_offset=None, in_=p_d,
                        in_offset=bass.IndirectOffsetOnAxis(ap=src_x[s][:, k:k + 1], axis=0)).then_inc(gathered[s], 16)
                    nc.gpsimd.indirect_dma_start(
                        out=q_g[s][:, k, :], out_offset=None, in_=q_d,
                        in_offset=bass.IndirectOffsetOnAxis(ap=dst_x[s][:, k:k + 1], axis=0)).then_inc(gathered[s], 16)
                    pool.wait_ge(scattered, t * 16 + 16)
                    pool.sem_inc(tiles_begun, 1)
                    nc.gpsimd.indirect_dma_start(
                        out=adj_d, out_offset=bass.IndirectOffsetOnAxis(ap=adj_x[s][:, k:k + 1], axis=0),
                        in_=w_sum[s][:, k:k + 1], in_offset=None, compute_op=ALU.add).then_inc(scattered, 16)

            with nc.gpsimd.Fori(0, BODY) as i:
                for s in range(SLOTS):
                    group(i, s)

        @block.scalar
        def _(act):
            def message(i, s):
                act.wait_ge(pre_ready, i * SLOTS + (s + 1))
                nc.scalar.activation(msg[s], pre[s], ACT.Silu).then_inc(msg_done, 1)
                act.wait_ge(msg_done, i * SLOTS + (s + 1))
                nc.scalar.activation(msg16[s][:, :, 0:C], msg[s], ACT.Copy).then_inc(msg_hi_ready, 1)

            with nc.scalar.Fori(0, BODY) as i:
                for s in range(SLOTS):
                    message(i, s)
            act.wait_ge(out0_ready, 1)
            for c, (d0, nd) in enumerate(CHUNKS):
                if c >= 2:
                    act.wait_ge(out0_turned, c - 1)
                nc.scalar.activation(halves_sb[c % 2][:, 0:nd], ps[c][:, 0:nd], ACT.Copy).then_inc(out0_copied, 1)
            act.wait_ge(h1_ready, 1)
            nc.scalar.activation(hh[0][0][:, :, 0:C], norm_c, ACT.Copy, scale=H_UP).then_inc(hi_ready, 1)
            act.wait_ge(hh_ready, NC)
            for k, (c, q, j0, nj) in enumerate(SPLITS):
                nd = CHUNKS[c][1]
                act.wait_ge(adj_loaded[k % 2], 16 * (k // 2 + 1))
                if (c, q) in streamed_of and streamed_of[c, q] >= 2:
                    act.wait_ge(unit_stored, 16 * (streamed_of[c, q] - 1))
                nc.scalar.activation(split_out(c, q)[:, :, 0, :],
                                     stage[k % 2][:, 0:nj * nd].rearrange("p (j d) -> p j d", d=nd),
                                     ACT.Copy, scale=A_HI).then_inc(adj_hi_ready, 1)
                if k >= 1 and SPLITS[k - 1][:2] in streamed_of:
                    v = streamed_of[SPLITS[k - 1][:2]]
                    act.wait_ge(adj_split, k)
                    if v:
                        act.wait_ge(unit_stored, 16 * v)
                    nc.scalar.dma_start(split_d[v], ring[v % 2].rearrange("p j h d -> p (j h d)")
                                        ).then_inc(unit_stored, 16)
            act.wait_ge(unit_stored, 16 * STREAMED)
            act.sem_inc(bank_free, NC)
            with nc.scalar.Fori(0, LAYERS // 2) as i:
                for half in range(2):
                    for c, (d0, nd) in enumerate(CHUNKS):
                        k = i * (2 * NC) + (half * NC + c)
                        b = (half * NC + c) % 2
                        w = nd // P * C
                        act.wait_ge(product_ready, k + 1)
                        nc.scalar.activation(halves_sb[b][:, 0:nd], ps[ACC[c]][:, 0:nd], ACT.Copy,
                                             scale=UNSCALE).then_inc(bank_free, 1)
                        act.wait_ge(turned, k + 1)
                        nc.scalar.activation(square[:, 0:w], ps[TURN[c]][0:P, 0:w], ACT.Square).then_inc(squared, 1)
                        act.wait_ge(eps_ready, k + 1)
                        nc.scalar.activation(n_tanh[b][:, 0:nd // P], n_eps[b][:, 0:nd // P],
                                             ACT.Tanh).then_inc(tanh_ready, 1)
                        act.wait_ge(new_ready, k + 1)
                        nc.scalar.activation(
                            hh[1 - half][0][:, d0 // P:(d0 + nd) // P, 0:C],
                            h_new[:, 0:w].rearrange("p (j c) -> p j c", c=C), ACT.Copy,
                            scale=H_UP).then_inc(hi_ready, 1)

        @block.vector
        def _(dve):
            done = [0]

            def link(ins):
                done[0] += 1
                ins.then_inc(dve_step, 1)
                dve.wait_ge(dve_step, done[0])

            def rsqrt(did, y, t, v):
                yi = y.bitcast(I32)
                did(nc.vector.tensor_scalar(yi, v.bitcast(I32), 1, None, ALU.logical_shift_right))
                did(nc.vector.tensor_scalar(yi, yi, -1.0, RSQRT_MAGIC, ALU.mult, ALU.add))
                for _ in range(3):
                    did(nc.vector.scalar_tensor_tensor(out=t, in0=y, scalar=-0.5, in1=y, op0=ALU.mult, op1=ALU.mult))
                    did(nc.vector.tensor_tensor(t, t, v, ALU.mult))
                    did(nc.vector.scalar_tensor_tensor(out=y, in0=t, scalar=1.5, in1=y, op0=ALU.add, op1=ALU.mult))

            def layernorm_relu(x, out, sq):
                mean, var, neg, rstd = (s[:, :] for s in stat)
                wide = (lambda v: v.unsqueeze(2).to_broadcast([P, NJ, C]))
                link(nc.vector.tensor_reduce(out=mean, in_=x, axis=AX.X, op=ALU.add))
                link(nc.vector.tensor_scalar(neg, mean, -1.0 / C, None, ALU.mult))
                link(nc.vector.tensor_tensor(out, x, wide(neg), ALU.add))
                link(nc.vector.tensor_tensor(sq, out, out, ALU.mult))
                link(nc.vector.tensor_reduce(out=var, in_=sq, axis=AX.X, op=ALU.add))
                link(nc.vector.tensor_scalar(neg, var, 1.0 / C, LN_EPS, ALU.mult, ALU.add))
                rsqrt(link, rstd, mean, neg)
                link(nc.vector.tensor_tensor(sq, out, wide(rstd), ALU.mult))
                return nc.vector.tensor_scalar(out, sq, 0.0, None, ALU.max)

            dve.sem_inc(keyrow_free, SLOTS)
            nc.vector.memset(zeros, 0.0).then_inc(zeros_ready, 1)
            nc.vector.memset(zeros16, 0.0).then_inc(zeros_ready, 1)
            dve.wait_ge(x_loaded, 16)
            layernorm_relu(z_acc[:], norm_c, norm_s).then_inc(h0_ready, 1)
            dve.wait_ge(iotas_ready, 4)
            link(nc.vector.tensor_scalar(ident, iota_sq, 0.0, None, ALU.is_equal))
            nc.vector.tensor_scalar(before, iota_sq, 0.0, None, ALU.is_lt)
            nc.vector.tensor_scalar(fold_b, iota_fold, -float(C), None, ALU.is_equal)
            link(nc.vector.tensor_scalar(fold[:], iota_fold, 0.0, None, ALU.is_equal))
            link(nc.vector.tensor_tensor(fold[:], fold[:], fold_b, ALU.add))
            dve.sem_inc(ident_ready, 1)
            dve.wait_ge(edges_loaded, 48)
            link(nc.vector.tensor_copy(src_f, src_i))
            link(nc.vector.scalar_tensor_tensor(out=key_f, in0=src_f, scalar=float(N), in1=dst_i,
                                                op0=ALU.mult, op1=ALU.add))
            dve.sem_inc(key_ready, 1)
            link(nc.vector.tensor_scalar(w_up, w_up, W_UP, None, ALU.mult))
            link(nc.vector.tensor_copy(stat[0][:, 0:1], spare_i))
            link(nc.vector.tensor_scalar(to_spare, key_f, -1.0, stat[0][:, 0:1], ALU.mult, ALU.add))
            for k in range(3):
                na = min(4, G - 4 * k)
                dve.wait_ge(key_turned, k + 1)
                nc.vector.tensor_copy(key_t[0:T // G, 4 * k:4 * k + na, :],
                                      ps[k][0:T // G, 0:na * P].rearrange("q (a p) -> q a p", p=P)
                                      ).then_inc(key_t_copied, 1)
            dve.wait_ge(bn_loaded, 64)
            link(nc.vector.tensor_scalar(bias, bn[:, 3, :], BN_EPS, None, ALU.add))
            rsqrt(link, inv, bn[:, 3, :], bias)
            link(nc.vector.tensor_tensor(inv, inv, bn[:, 0, :], ALU.mult))
            link(nc.vector.tensor_tensor(bias, inv, bn[:, 2, :], ALU.mult))
            link(nc.vector.tensor_tensor(bias, bn[:, 1, :], bias, ALU.subtract))
            dve.wait_ge(w_turned, 1)
            link(nc.vector.tensor_copy(w_t[0:C, :], ps[3][0:C, 0:2 * C]))
            link(nc.vector.tensor_tensor(w_t[0:C, 0:C], w_t[0:C, 0:C], w_t[0:C, C:2 * C], ALU.subtract))
            nc.vector.tensor_tensor(w_fold[0:C, 0:C], w_t[0:C, 0:C], inv[0:C], ALU.mult).then_inc(w_folded, 1)
            nc.vector.tensor_tensor(w_fold[0:C, C:2 * C], w_t[0:C, C:2 * C], inv[0:C], ALU.mult).then_inc(w_folded, 1)
            for c, (d0, nd) in enumerate(CHUNKS):
                dve.wait_ge(h0_turned, c + 1)
                nc.vector.tensor_copy(h0t[0:C, d0:d0 + nd], ps[4 + c % 2][0:C, 0:nd]).then_inc(h0t_copied, 1)
            for c, (d0, nd) in enumerate(CHUNKS):
                dve.wait_ge(pq_made, c + 1)
                nj = nd // P
                got = ps[6 + c % 2][0:P, 0:nj * 2 * C].rearrange("p (j c) -> p j c", c=2 * C)
                nc.vector.tensor_tensor(pq[:, d0 // P:d0 // P + nj, 0:C], got[:, :, 0:C],
                                        bias.unsqueeze(1).to_broadcast([P, nj, C]), ALU.add)
                link(nc.vector.tensor_copy(pq[:, d0 // P:d0 // P + nj, C:2 * C], got[:, :, C:2 * C]))
                dve.sem_inc(pq_copied, 1)
            dve.sem_inc(pq_ready, 1)

            PREP, USE = 9, 1
            base0 = done[0]

            def prep(g, slot_turn, s, step0):
                step = [0]

                def did(ins):
                    step[0] += 1
                    ins.then_inc(dve_step, 1)
                    dve.wait_ge(dve_step, step0 + step[0])

                cols = bass.ds(g * G, G)
                dve.wait_ge(tiles_begun, g * G + 1)
                did(nc.vector.tensor_copy(w_c[s], w_up[:, cols]))
                dve.wait_ge(keyrow_loaded[s], slot_turn * 16 + 16)
                did(nc.vector.tensor_tensor(equal, keyrow[s], key_f[:, cols].unsqueeze(2).to_broadcast([P, G, P]),
                                            ALU.is_equal))
                dve.sem_inc(keyrow_free, 1)
                did(nc.vector.tensor_tensor(repeat[s], equal, before.unsqueeze(1).to_broadcast([P, G, P]), ALU.mult))
                dve.sem_inc(repeat_ready, 1)
                did(nc.vector.tensor_reduce(out=count, in_=repeat[s], axis=AX.X, op=ALU.add))
                did(nc.vector.scalar_tensor_tensor(out=shift, in0=count, scalar=1.0, in1=to_spare[:, cols],
                                                   op0=ALU.min, op1=ALU.mult))
                nc.vector.tensor_copy(src_x[s], src_i[:, cols])
                nc.vector.tensor_copy(dst_x[s], dst_i[:, cols])
                did(nc.vector.tensor_copy(src_c[s], src_f[:, cols]))
                did(nc.vector.tensor_tensor(adj_x[s], shift, key_f[:, cols], ALU.add))
                dve.wait_ge(repeat_summed, g + 1)
                did(nc.vector.tensor_tensor(w_sum[s], w_c[s], ps[7][0:P, 0:G], ALU.add))
                dve.sem_inc(prep_ready, 1)
                assert step[0] == PREP - 1

            def use(g, slot_turn, s, step0):
                dve.wait_ge(gathered[s], slot_turn * (32 * G) + 32 * G)
                nc.vector.tensor_tensor(pre[s], p_g[s], q_g[s], ALU.add).then_inc(pre_ready, 1)
                for k in range(G):
                    t = g * G + k
                    if k == OH:
                        dve.wait_ge(msg_hi_ready, g + 1)
                        nc.vector.tensor_tensor(msg16[s][:, :, C:2 * C], msg[s], msg16[s][:, :, 0:C],
                                                ALU.subtract).then_inc(msg_ready, 1)
                    dve.wait_ge(onehot_free, t + 1)
                    nc.vector.tensor_scalar(onehot[(s * G + k) % OH], iota16, src_c[s][:, k:k + 1], None,
                                            ALU.is_equal).then_inc(onehot_ready, 1)

            S = PREP - 1
            prep(0, 0, 0, base0)
            with nc.vector.Fori(0, BODY - 1) as i:
                for s in range(SLOTS):
                    n = (s + 1) % SLOTS
                    prep(i * SLOTS + (s + 1), i + (s + 1) // SLOTS, n, i * (S * SLOTS) + (base0 + S * (s + 1)))
                    use(i * SLOTS + s, i, s, None)
            for s in range(SLOTS):
                g = (BODY - 1) * SLOTS + s
                if g + 1 < NG:
                    prep(g + 1, (g + 1) // SLOTS, (s + 1) % SLOTS, base0 + S * (g + 1))
                use(g, g // SLOTS, s, None)
            done[0] = base0 + S * NG

            for c, (d0, nd) in enumerate(CHUNKS):
                nj = nd // P
                v = z_acc[:, d0 // P:d0 // P + nj, :]
                dve.wait_ge(out0_turned, c + 1)
                nc.vector.tensor_tensor(v, v, ps[c][0:P, 0:nj * C].rearrange("p (j c) -> p j c", c=C),
                                        ALU.add).then_inc(out0_added, 1)
            dve.wait_ge(out0_added, NC)
            link(layernorm_relu(z_acc[:], norm_c, norm_s))
            dve.sem_inc(h1_ready, 1)
            dve.wait_ge(mix_loaded, 16)
            link(nc.vector.scalar_tensor_tensor(out=z_acc[:], in0=norm_c, scalar=mix[:, 0:1], in1=z_acc[:],
                                                op0=ALU.mult, op1=ALU.add))
            dve.wait_ge(hi_ready, 1)
            link(nc.vector.scalar_tensor_tensor(out=hh[0][0][:, :, C:2 * C], in0=norm_c, scalar=H_UP,
                                                in1=hh[0][0][:, :, 0:C], op0=ALU.mult, op1=ALU.subtract))
            link(nc.vector.tensor_scalar(hh[0][1], hh[0][0], A_HI, None, ALU.mult))
            dve.sem_inc(hh_ready, NC)
            for k, (c, q, j0, nj) in enumerate(SPLITS):
                nd = CHUNKS[c][1]
                dve.wait_ge(adj_hi_ready, k + 1)
                o = split_out(c, q)
                nc.vector.scalar_tensor_tensor(out=o[:, :, 1, :], in0=o[:, :, 0, :], scalar=-1.0 / A_HI,
                                               in1=stage[k % 2][:, 0:nj * nd].rearrange("p (j d) -> p j d", d=nd),
                                               op0=ALU.mult, op1=ALU.add).then_inc(adj_split, 1)
                dve.wait_ge(adj_split, k + 1)
                dve.sem_inc(stage_free, 1)

            base1 = done[0]
            STEPS = 17
            with nc.vector.Fori(0, LAYERS // 2) as i:
                for half in range(2):
                    layer = i * 2 + (half + 1)
                    for c, (d0, nd) in enumerate(CHUNKS):
                        kk = half * NC + c
                        k = i * (2 * NC) + kk
                        b = kk % 2
                        nj = nd // P
                        w = nj * C
                        step = [0]

                        def did(ins):
                            step[0] += 1
                            ins.then_inc(dve_step, 1)
                            dve.wait_ge(dve_step, i * (2 * NC * STEPS) + (base1 + kk * STEPS + step[0]))

                        new = h_new[:, 0:w].rearrange("p (j c) -> p j c", c=C)
                        dve.wait_ge(squared, k + 1)
                        did(nc.vector.tensor_reduce(out=n_sq[b][:, 0:nj],
                                                    in_=square[:, 0:w].rearrange("p (j c) -> p j c", c=C),
                                                    axis=AX.X, op=ALU.add))
                        rsqrt(did, factor[b][:, 0:nj], n_eps[b][:, 0:nj], n_sq[b][:, 0:nj])
                        did(nc.vector.tensor_tensor(n_tanh[b][:, 0:nj], factor[b][:, 0:nj], n_sq[b][:, 0:nj],
                                                    ALU.mult))
                        nc.vector.tensor_scalar(n_eps[b][:, 0:nj], n_tanh[b][:, 0:nj], NORM_EPS, None,
                                                ALU.add).then_inc(eps_ready, 1)
                        dve.wait_ge(eps_ready, k + 1)
                        did(nc.vector.reciprocal(n_sq[b][:, 0:nj], n_eps[b][:, 0:nj]))
                        dve.wait_ge(tanh_ready, k + 1)
                        did(nc.vector.tensor_tensor(factor[b][:, 0:nj], n_tanh[b][:, 0:nj], n_sq[b][:, 0:nj],
                                                    ALU.mult))
                        nc.vector.tensor_tensor(new, ps[TURN[c]][0:P, 0:w].rearrange("p (j c) -> p j c", c=C),
                                                factor[b][:, 0:nj].unsqueeze(2).to_broadcast([P, nj, C]),
                                                ALU.mult).then_inc(new_ready, 1)
                        dve.wait_ge(new_ready, k + 1)
                        zc = z_acc[:, d0 // P:d0 // P + nj, :]
                        nc.vector.scalar_tensor_tensor(out=zc, in0=new, scalar=mix[:, bass.ds(layer, 1)], in1=zc,
                                                       op0=ALU.mult, op1=ALU.add)
                        dve.wait_ge(hi_ready, k + 2)
                        hi = hh[1 - half][0][:, d0 // P:d0 // P + nj, :]
                        did(nc.vector.scalar_tensor_tensor(out=hi[:, :, C:2 * C], in0=new, scalar=H_UP,
                                                           in1=hi[:, :, 0:C], op0=ALU.mult, op1=ALU.subtract))
                        did(nc.vector.tensor_scalar(hh[1 - half][1][:, d0 // P:d0 // P + nj, :], hi, A_HI, None,
                                                    ALU.mult))
                        dve.sem_inc(hh_ready, 1)
                        assert step[0] == STEPS

        @block.tensor
        def _(pe):
            pe.wait_ge(ident_ready, 1)
            pe.wait_ge(key_ready, 1)
            for k in range(3):
                for a in range(4 * k, min(4 * k + 4, G)):
                    last = nc.tensor.transpose(ps[k][0:T // G, (a % 4) * P:(a % 4 + 1) * P],
                                               key_f[:, a * (T // G):(a + 1) * (T // G)], ident)
                last.then_inc(key_turned, 1)
            pe.wait_ge(w_loaded, 16)
            for h in range(2):
                last = nc.tensor.transpose(ps[3][0:C, h * C:(h + 1) * C], w_nat[0:C, h * C:(h + 1) * C],
                                           ident[0:C, 0:C])
            last.then_inc(w_turned, 1)
            pe.wait_ge(h0_ready, 1)
            for c, (d0, nd) in enumerate(CHUNKS):
                if c >= 2:
                    pe.wait_ge(h0t_copied, c - 1)
                for u in range(nd // P):
                    last = nc.tensor.transpose(ps[4 + c % 2][0:C, u * P:(u + 1) * P], norm_c[:, d0 // P + u, :], ident)
                last.then_inc(h0_turned, 1)
            pe.wait_ge(w_folded, 2)
            pe.wait_ge(h0t_copied, NC)
            for c, (d0, nd) in enumerate(CHUNKS):
                if c >= 2:
                    pe.wait_ge(pq_copied, c - 1)
                for u in range(nd // P):
                    last = nc.tensor.matmul(ps[6 + c % 2][0:P, u * 2 * C:(u + 1) * 2 * C],
                                            h0t[0:C, d0 + u * P:d0 + (u + 1) * P], w_fold[0:C, :],
                                            start=True, stop=True)
                last.then_inc(pq_made, 1)

            pe.wait_ge(zeros_ready, 2)
            pe.wait_ge(pq_ready, 1)
            for c, (d0, nd) in enumerate(CHUNKS):
                nc.tensor.matmul(ps[c][:, 0:nd], zeros16[:, 0:128], zeros16[:, 128:128 + nd], start=True, stop=False)
            pe.sem_inc(onehot_free, OH)

            def sum_repeats(g, s):
                pe.wait_ge(repeat_ready, g + 1)
                for k in range(G):
                    last = nc.tensor.matmul(ps[7][0:P, k:k + 1], repeat[s][:, k, :], w_c[s][:, k:k + 1],
                                            start=True, stop=True)
                last.then_inc(repeat_summed, 1)

            def add_messages(g, s):
                pe.wait_ge(msg_ready, g + 1)
                for k in range(G):
                    pe.wait_ge(onehot_ready, g * G + (k + 1))
                    for c, (d0, nd) in enumerate(CHUNKS):
                        last = nc.tensor.matmul(ps[c][:, 0:nd], msg16[s][:, k, :],
                                                onehot[(s * G + k) % OH][:, d0:d0 + nd], start=False, stop=False)
                    last.then_inc(onehot_free, 1)

            sum_repeats(0, 0)
            with nc.tensor.Fori(0, BODY - 1) as i:
                for s in range(SLOTS):
                    sum_repeats(i * SLOTS + (s + 1), (s + 1) % SLOTS)
                    add_messages(i * SLOTS + s, s)
            for s in range(SLOTS):
                g = (BODY - 1) * SLOTS + s
                if g + 1 < NG:
                    sum_repeats(g + 1, (s + 1) % SLOTS)
                add_messages(g, s)
            for c, (d0, nd) in enumerate(CHUNKS):
                last = nc.tensor.matmul(ps[c][:, 0:nd], zeros16[:, 0:128], zeros16[:, 128:128 + nd],
                                        start=False, stop=True)
            last.then_inc(out0_ready, 1)
            for c, (d0, nd) in enumerate(CHUNKS):
                pe.wait_ge(out0_copied, c + 1)
                for u in range(nd // P):
                    last = nc.tensor.matmul(ps[c][0:P, u * C:(u + 1) * C], halves_sb[c % 2][:, u * P:(u + 1) * P],
                                            fold[:], start=True, stop=True)
                last.then_inc(out0_turned, 1)

            pe.sem_inc(unit_used, RING)
            pe.wait_ge(adj_split, len(SPLITS))

            def turn(c, k, b):
                pe.wait_ge(bank_free, k + (NC + 1))
                for u in range(CHUNKS[c][1] // P):
                    last = nc.tensor.matmul(ps[TURN[c]][0:P, u * C:(u + 1) * C], halves_sb[b][:, u * P:(u + 1) * P],
                                            fold[:], start=True, stop=True)
                last.then_inc(turned, 1)

            with nc.tensor.Fori(0, LAYERS // 2) as i:
                for half in range(2):
                    for c, (d0, nd) in enumerate(CHUNKS):
                        kk = half * NC + c
                        k = i * (2 * NC) + kk
                        pe.wait_ge(bank_free, k + (NC + 1 - (3 if 3 <= c < NC - 1 else 4 if c < 3 else NC)))
                        for j in range(NJ):
                            if c == 0 and j % BPC == 0:
                                pe.wait_ge(hh_ready, i * (2 * NC) + (half * NC + j // BPC + 1))
                            q, jj = j // UJ, j % UJ
                            if c == NC - 1:
                                q, a = 0, last_adj[:, j]
                            elif (c, q) in resident_of:
                                a = res[resident_of[c, q]][:, jj]
                            else:
                                v = half * STREAMED + streamed_of[c, q]
                                a = ring[v % RING][:, jj]
                                if jj == 0:
                                    pe.wait_ge(streamed[v % RING],
                                               i * (2 * STREAMED // RING * 16) + 16 * (v // RING + 1))
                            for part in range(2):
                                last = nc.tensor.matmul(ps[ACC[c]][:, 0:nd], hh[half][part][:, j, :], a[:, part, :],
                                                        start=(j == 0 and part == 0),
                                                        stop=(j == NJ - 1 and part == 1))
                            if (c, q) in streamed_of and jj == UJ - 1:
                                last.then_inc(unit_used, 1)
                            if j == 12 and c > 0:
                                turn(c - 1, k - 1, (kk - 1) % 2)
                        last.then_inc(product_ready, 1)
                    turn(NC - 1, k, kk % 2)


ACC = [0, 1, 2, 0, 1, 2, 3]
TURN = [4, 5, 6, 4, 5, 6, 7]


_INS = ['x', 'src', 'dst', 'edge_weight', 'L0_gnn_W', 'L0_gnn_bn_gamma', 'L0_gnn_bn_beta', 'L0_gnn_bn_mean',
        'L0_gnn_bn_var', 'L1_gnn_manifold_weights']


def kernel(**inputs):
    import numpy as _np
    import concourse.bacc as _bacc
    from concourse import mybir as _mybir
    from concourse.bass_utils import run_bass_kernel_spmd as _run

    nc = _bacc.Bacc("TRN2", target_bir_lowering=False, num_devices=1)
    arrays, args = {}, []
    for name in _INS:
        a = _np.ascontiguousarray(inputs[name])
        arrays[f"in_{name}_dram"] = a
        args.append(nc.dram_tensor(f"in_{name}_dram", a.shape, _mybir.dt.from_np(a.dtype), kind="ExternalInput").ap())
    args.append(nc.dram_tensor("out_0_dram", (N, C), _mybir.dt.float32, kind="ExternalOutput").ap())
    gnn_kernel(nc, *args)
    r = _run(nc, [arrays], core_ids=[0])
    return r.results[0]["out_0_dram"]
```

```python
from contextlib import ExitStack

import concourse.bass as bass
from concourse import mybir

F32 = mybir.dt.float32
F16 = mybir.dt.float16
I32 = mybir.dt.int32
I16 = mybir.dt.int16
ALU = mybir.AluOpType
ACT = mybir.ActivationFunctionType
AX = mybir.AxisListType

N = 3125
C = 64
P = 125
NJ = N // P
E = 103125
T = E // P
G = 11
SLOTS = 3
NG = T // G
BODY = NG // SLOTS
OH = 3
BUNDLES = [tuple(range(k, min(k + 2, G))) for k in range(0, G, 2)]
NB = len(BUNDLES)
PIECES = [(0, 6), (6, G)]
WINDOW = P
TROWS = T // G
Q_UP = 256.0
CHUNK = 500
BPC = CHUNK // P
CHUNKS = [(c * CHUNK, min(CHUNK, N - c * CHUNK)) for c in range(-(-N // CHUNK))]
NC = len(CHUNKS)
LAYERS = 10
UJ = 5
NQ = NJ // UJ
RESIDENT = (1, 4)
STREAMED = (NC - 1) * (NQ - len(RESIDENT))
RING = 3
LN_EPS = 1e-5
BN_EPS = 1e-5
NORM_EPS = 1e-8
W_UP = 512.0
RSQRT_MAGIC = float(0x5F3759DF)
A_HI = 2.0 ** -11
H_UP = 4096.0
UNSCALE = 1.0 / (W_UP * A_HI * H_UP)


def gnn_kernel(nc, x_d, src_d, dst_d, ew_d, w_d, gamma_d, beta_d, mean_d, var_d, mix_d, out_d):
    p_d = nc.dram_tensor("p_rows", (N, C), F32, kind="Internal").ap()
    q_d = nc.dram_tensor("q_rows", (N + 1, C), F32, kind="Internal").ap()
    q16_d = nc.dram_tensor("q_halves", (N, 2 * C), F16, kind="Internal").ap()
    key_d = nc.dram_tensor("key_rows", (T, P), F32, kind="Internal").ap()
    adj_d = nc.dram_tensor("adjacency", (N * N + 2 * P, 1), F32, kind="Internal").ap()
    adj_rows = adj_d[0:N * N, :].rearrange("(j p d) o -> p j (d o)", p=P, d=N)
    split_d = nc.dram_tensor("split_units", (STREAMED, P, UJ * 2 * CHUNK), F16, kind="Internal").ap()

    ctx = ExitStack()
    with ctx:
        def sb(name, shape, dt):
            return ctx.enter_context(nc.sbuf_tensor(name, shape, dt))

        def sem(name):
            return ctx.enter_context(nc.semaphore(name))

        ps = [ctx.enter_context(nc.psum_tensor(f"bank{b}", [128, 512], F32)) for b in range(8)]

        z_acc = sb("z_acc", [P, NJ, C], F32)
        mix = sb("mix", [P, LAYERS + 1], F32)
        fold = sb("fold", [128, C], F32)
        hh_all = sb("hh_all", [P, 4, NJ, 2 * C], F16)
        hh = [[hh_all[:, 2 * a + s] for s in range(2)] for a in range(2)]
        stage0 = sb("stage0", [P, UJ * CHUNK], F32)
        UNIT = UJ * 2 * CHUNK
        LAST = NJ * 2 * P
        n_res = (NC - 1) * len(RESIDENT)
        ARENA = (n_res + RING) * UNIT + LAST
        arena = sb("arena", [P, ARENA], F16)
        res = [arena[:, k * UNIT:(k + 1) * UNIT].rearrange("p (j h d) -> p j h d", j=UJ, h=2) for k in range(n_res)]
        last_adj = arena[:, n_res * UNIT:n_res * UNIT + LAST].rearrange("p (j h d) -> p j h d", j=NJ, h=2)
        ring = [arena[:, n_res * UNIT + LAST + k * UNIT:n_res * UNIT + LAST + (k + 1) * UNIT]
                .rearrange("p (j h d) -> p j h d", j=UJ, h=2) for k in range(RING)]
        stage = [stage0[:, :], arena[:, ARENA - UNIT:ARENA].bitcast(F32)]
        at = [0]

        def carve(shape, dt):
            n = 1
            for s in shape:
                n *= s
            halves = n if dt in (F16, I16) else 2 * n
            at[0] += at[0] % 2
            v = arena[:, at[0]:at[0] + halves]
            at[0] += halves
            assert at[0] <= ARENA
            v = v if dt == F16 else v.bitcast(dt)
            if len(shape) == 2:
                v = v.rearrange("p (a b) -> p a b", b=shape[1])
            return v

        src_f = carve([T], F32)
        dst_f = carve([T], F32)
        w_up = carve([T], F32)
        key_f = carve([T], F32)
        to_spare = carve([T], F32)
        in_window = carve([T], F32)
        cols = carve([T], F32)
        q_index = carve([T], I32)
        w16 = carve([T, 2], F16)
        window_node = carve([NG], F32)
        first_node = carve([NG], F32)
        first_i = carve([NG], I32)
        outside = carve([NG], I32)
        iota16 = carve([N + 1], I16)
        onehot = [carve([N + 1], F16) for _ in range(OH)]
        ident = carve([P], F32)
        ones = carve([P], F32)
        before = carve([2, P], F16)
        iota_sq = carve([P], I32)
        spare_i = carve([1], I32)
        spare_f = carve([1], F32)
        row_f = carve([1], F32)
        rows_at = at[0]
        keyrow = [carve([G, P], F32) for _ in range(SLOTS)]
        dstrow = [carve([G, P], I32) for _ in range(SLOTS)]
        rows = [arena[:, rows_at + k * 2 * G * P:rows_at + (k + 1) * 2 * G * P].bitcast(F32)
                .rearrange("p (a b) -> p a b", b=P) for k in range(6)]
        src_row_i, dst_row_i, w_row, src_row, dst_row, key_row = rows
        src_row_i, dst_row_i = src_row_i.bitcast(I32), dst_row_i.bitcast(I32)
        pick_dst = [carve([G, P], F16) for _ in range(SLOTS)]
        REP = sum((2 * len(b) - 1) * P for b in BUNDLES)
        repeat = [carve([REP], F16) for _ in range(SLOTS)]
        count = carve([G], F32)
        shift = carve([G], F32)
        src_x = [carve([G], I32) for _ in range(SLOTS)]
        q_x = carve([G], I32)
        adj_x = [carve([G], I32) for _ in range(SLOTS)]
        src_c = [carve([G], F32) for _ in range(SLOTS)]
        key_c = carve([G], F32)
        node_c = carve([1], F32)
        w16_c = [carve([G, 2], F16) for _ in range(SLOTS)]
        later = [carve([2 * G], F32) for _ in range(SLOTS)]
        w_sum = [carve([G], F32) for _ in range(SLOTS)]
        q_window = [carve([2 * C], F16) for _ in range(SLOTS)]
        gathers_at = at[0]
        p_g = [carve([G, C], F32) for _ in range(SLOTS)]
        msg = [carve([G, C], F32) for _ in range(SLOTS)]
        norm_s = arena[:, gathers_at:gathers_at + 2 * NJ * C].bitcast(F32).rearrange("p (j c) -> p j c", c=C)
        h0t = arena[:, gathers_at:gathers_at + 2 * N].bitcast(F32)
        assert at[0] >= gathers_at + 2 * N
        msg16 = [carve([G, 2 * C], F16) for _ in range(SLOTS)]
        zeros = carve([N], F32)
        zeros16 = carve([128 + CHUNK], F16)
        norm_c = carve([NJ, C], F32)
        pq = hh_all[:, 0:2].rearrange("p a j c -> p (a j c)").bitcast(F32).rearrange("p (j c) -> p j c", c=2 * C)
        q16 = hh_all[:, 2]
        w_nat = carve([2 * C], F32)
        w_t = carve([2 * C], F32)
        w_fold = carve([2 * C], F32)
        bn = carve([4, C], F32)
        inv = carve([C], F32)
        bias = carve([C], F32)
        halves_sb = [sb(f"halves_sb{k}", [128, CHUNK], F32) for k in range(2)]
        stat = [sb(f"stat{k}", [P, NJ], F32) for k in range(4)]
        square = sb("square", [P, BPC * C], F32)
        h_new = sb("h_new", [P, BPC * C], F32)
        n_sq = [sb(f"n_sq{k}", [P, BPC], F32) for k in range(2)]
        n_eps = [sb(f"n_eps{k}", [P, BPC], F32) for k in range(2)]
        n_tanh = [sb(f"n_tanh{k}", [P, BPC], F32) for k in range(2)]
        factor = [sb(f"factor{k}", [P, BPC], F32) for k in range(2)]
        iota_fold = halves_sb[1][:, 0:C].bitcast(I32)
        fold_b = halves_sb[0][:, 0:C]

        edges_loaded, x_loaded, bn_loaded, mix_loaded, w_loaded = (
            sem(n) for n in ("edges_loaded", "x_loaded", "bn_loaded", "mix_loaded", "w_loaded"))
        iotas_ready, ident_ready, zeros_ready = sem("iotas_ready"), sem("ident_ready"), sem("zeros_ready")
        zero_filled = sem("zero_filled")
        key_ready, rows_turned, columns_copied, columns_ready, key_stored = (
            sem(n) for n in ("key_ready", "rows_turned", "columns_copied", "columns_ready", "key_stored"))
        firsts_ready, firsts_spread, inside_ready, inside_summed, windows_ready = (
            sem(n) for n in ("firsts_ready", "firsts_spread", "inside_ready", "inside_summed", "windows_ready"))
        window_made, window_out = sem("window_made"), sem("window_out")
        q_ready, q_step, q_landed = sem("q_ready"), sem("q_step"), sem("q_landed")
        h0_ready, h0_turned, h0t_copied = sem("h0_ready"), sem("h0_turned"), sem("h0t_copied")
        w_turned, w_folded, pq_made, pq_ready, pq_stored = (
            sem("w_turned"), sem("w_folded"), sem("pq_made"), sem("pq_ready"), sem("pq_stored"))
        dve_step = sem("dve_step")
        keyrow_loaded = [sem(f"keyrow_loaded{s}") for s in range(SLOTS)]
        gathered = [sem(f"gathered{s}") for s in range(SLOTS)]
        keyrow_free, bundles_begun, groups_begun, repeat_ready, repeat_out, prep_ready = (
            sem("keyrow_free"), sem("bundles_begun"), sem("groups_begun"), sem("repeat_ready"), sem("repeat_out"), sem("prep_ready"))
        scattered = sem("scattered")
        pre_ready, msg_hi_ready, msg_ready = sem("pre_ready"), sem("msg_hi_ready"), sem("msg_ready")
        msg_done = sem("msg_done")
        pq_copied = sem("pq_copied")
        onehot_ready, onehot_free = sem("onehot_ready"), sem("onehot_free")
        out0_ready, out0_copied, out0_turned, out0_added = (
            sem("out0_ready"), sem("out0_copied"), sem("out0_turned"), sem("out0_added"))
        h1_ready = sem("h1_ready")
        adj_loaded = [sem(f"adj_loaded{k}") for k in range(2)]
        adj_hi_ready, adj_split, stage_free = sem("adj_hi_ready"), sem("adj_split"), sem("stage_free")
        unit_stored = sem("unit_stored")
        streamed = [sem(f"streamed{k}") for k in range(RING)]
        unit_used = sem("unit_used")
        product_ready, bank_free, turned, squared, eps_ready, tanh_ready, new_ready, hi_ready, hh_ready = (
            sem(n) for n in ("product_ready", "bank_free", "turned", "squared", "eps_ready", "tanh_ready",
                             "new_ready", "hi_ready", "hh_ready"))
        out_stored = sem("out_stored")

        block = ctx.enter_context(nc.Block())

        units = [(c, q) for c in range(NC - 1) for q in range(NQ)]
        streamed_of = {}
        resident_of = {}
        for c, q in units:
            if q in RESIDENT:
                resident_of[c, q] = len(resident_of)
            else:
                streamed_of[c, q] = len(streamed_of)

        SPLITS = [(c, q, UJ * q, UJ) for c, q in units] + [(NC - 1, 0, 0, 20), (NC - 1, 1, 20, 5)]

        def split_out(c, q):
            if c == NC - 1:
                return last_adj[:, 20 * q:20 + 5 * q]
            return res[resident_of[c, q]] if (c, q) in resident_of else ring[streamed_of[c, q] % 2]

        @block.sync
        def _(sp):
            sp.dma_start(z_acc[:], x_d.rearrange("(j p) c -> p j c", p=P)).then_inc(x_loaded, 16)
            for dram, tile in ((src_d, src_row_i), (dst_d, dst_row_i), (ew_d, w_row)):
                sp.dma_start(tile[0:TROWS], dram.rearrange("(a q p) -> q a p", q=TROWS, p=P)
                             ).then_inc(edges_loaded, 16)
            sp.dma_start(w_nat[0:C, :], w_d).then_inc(w_loaded, 16)
            for k, dram in enumerate((gamma_d, beta_d, mean_d, var_d)):
                sp.dma_start(bn[:, k, :], dram.partition_broadcast(P)).then_inc(bn_loaded, 16)
            sp.dma_start(mix[:], mix_d.partition_broadcast(P)).then_inc(mix_loaded, 16)
            sp.wait_ge(key_ready, 1)
            sp.dma_start(key_d.rearrange("(a q) p -> q a p", q=TROWS), key_row[0:TROWS]).then_inc(key_stored, 16)
            sp.wait_ge(pq_ready, 1)
            sp.dma_start(p_d.rearrange("(j p) c -> p j c", p=P), pq[:, :, 0:C]).then_inc(pq_stored, 16)
            sp.dma_start(q_d[0:N, :].rearrange("(j p) c -> p j c", p=P), pq[:, :, C:2 * C]).then_inc(pq_stored, 16)
            sp.wait_ge(zeros_ready, 1)
            sp.dma_start(q_d[N:N + 1, :], zeros[0:1, 0:C]).then_inc(pq_stored, 16)
            sp.dma_start(q16_d.rearrange("(j p) c -> p j c", p=P), q16).then_inc(pq_stored, 16)
            sp.wait_ge(pq_stored, 64)
            sp.wait_ge(key_stored, 16)
            sp.wait_ge(columns_ready, 1)
            sp.wait_ge(windows_ready, 1)
            key_flat = key_d.rearrange("t p -> (t p)")
            with sp.Fori(0, BODY) as i:
                for s in range(SLOTS):
                    g = i * SLOTS + s
                    node = sp.value_load(first_i[0:1, bass.ds(g, 1)], min_val=0, max_val=N - WINDOW)
                    sp.wait_ge(keyrow_free, g + 1)
                    sp.dma_start(keyrow[s].rearrange("p a b -> p (a b)"),
                                 key_flat[bass.ds(g * (G * P), G * P)].partition_broadcast(P)
                                 ).then_inc(keyrow_loaded[s], 16)
                    sp.dma_start(dstrow[s].rearrange("p a b -> p (a b)"),
                                 dst_d[bass.ds(g * (G * P), G * P)].partition_broadcast(P)
                                 ).then_inc(keyrow_loaded[s], 16)
                    sp.wait_ge(window_out, g * 2 + 2)
                    sp.dma_start(q_window[s][0:WINDOW, :], q16_d[bass.ds(node, WINDOW), :]).then_inc(keyrow_loaded[s], 16)
            sp.wait_ge(scattered, 16 * T + 16)
            sp.wait_ge(hh_ready, NC)
            for k, (c, q, j0, nj) in enumerate(SPLITS):
                d0, nd = CHUNKS[c]
                if k >= 2:
                    sp.wait_ge(stage_free, k - 1)
                sp.dma_start(stage[k % 2][:, 0:nj * nd].rearrange("p (j d) -> p j d", d=nd),
                             adj_rows[:, j0:j0 + nj, d0:d0 + nd]).then_inc(adj_loaded[k % 2], 16)
            sp.wait_ge(unit_stored, 16 * STREAMED)
            sp.wait_ge(stage_free, len(SPLITS))
            with sp.Fori(0, LAYERS // 2) as i:
                for v in range(2 * STREAMED):
                    sp.wait_ge(unit_used, i * (2 * STREAMED) + (v + 1))
                    sp.dma_start(ring[v % RING].rearrange("p j h d -> p (j h d)"),
                                 split_d[v % STREAMED]).then_inc(streamed[v % RING], 16)
            sp.wait_ge(hh_ready, NC * (LAYERS + 1))
            sp.dma_start(out_d.rearrange("(j p) c -> p j c", p=P), z_acc[:]).then_inc(out_stored, 16)
            sp.wait_ge(out_stored, 16)

        @block.gpsimd
        def _(pool):
            nc.gpsimd.iota(iota16, pattern=[[1, N + 1]], base=0, channel_multiplier=0).then_inc(iotas_ready, 1)
            nc.gpsimd.iota(iota_sq, pattern=[[1, P]], base=0, channel_multiplier=-1).then_inc(iotas_ready, 1)
            nc.gpsimd.iota(spare_i, pattern=[[1, 1]], base=N * N, channel_multiplier=1).then_inc(iotas_ready, 1)
            nc.gpsimd.iota(iota_fold, pattern=[[1, C]], base=0, channel_multiplier=-1).then_inc(iotas_ready, 1)
            pool.sem_inc(bundles_begun, 2 * NB)
            pool.wait_ge(zeros_ready, 1)
            nc.gpsimd.dma_start(adj_d[N * N:N * N + 2 * P, :].rearrange("(p a) o -> p (a o)", a=2), zeros[:, 0:2]
                                ).then_inc(scattered, 16)
            pool.wait_ge(pq_stored, 64)
            pool.wait_ge(windows_ready, 1)
            pool.wait_ge(zero_filled, 16 * NJ)

            def group(i, s):
                pool.wait_ge(prep_ready, i * SLOTS + (s + 1))
                pool.sem_inc(groups_begun, 1)
                for bundle in BUNDLES:
                    for k in bundle:
                        nc.gpsimd.indirect_dma_start(
                            out=p_g[s][:, k, :], out_offset=None, in_=p_d,
                            in_offset=bass.IndirectOffsetOnAxis(ap=src_x[s][:, k:k + 1], axis=0)
                        ).then_inc(gathered[s], 16)
                    pool.wait_ge(scattered, i * (SLOTS * G * 16) + (s * G + bundle[0]) * 16 + 16)
                    pool.sem_inc(bundles_begun, 1)
                    for k in bundle:
                        nc.gpsimd.indirect_dma_start(
                            out=adj_d, out_offset=bass.IndirectOffsetOnAxis(ap=adj_x[s][:, k:k + 1], axis=0),
                            in_=w_sum[s][:, k:k + 1], in_offset=None, compute_op=ALU.add).then_inc(scattered, 16)
                g = i * SLOTS + s
                some_outside = pool.value_load(outside[0:1, bass.ds(g, 1)], min_val=0, max_val=G * P)
                with pool.If(some_outside > 0):
                    nc.gpsimd.tensor_copy(q_x, q_index[:, bass.ds(g * G, G)]).then_inc(q_step, 1)
                    pool.wait_ge(q_step, 1)
                    pool.sem_clear(q_step)
                    pool.wait_ge(gathered[s], i * (16 * G) + 16 * G)
                    pool.sem_inc(groups_begun, 1)
                    for k in range(G):
                        nc.gpsimd.indirect_dma_start(
                            out=p_g[s][:, k, :], out_offset=None, in_=q_d,
                            in_offset=bass.IndirectOffsetOnAxis(ap=q_x[:, k:k + 1], axis=0),
                            compute_op=ALU.add).then_inc(q_landed, 16)
                    pool.wait_ge(q_landed, 16 * G)
                    pool.sem_clear(q_landed)
                pool.sem_inc(q_ready, 1)

            with nc.gpsimd.Fori(0, BODY) as i:
                for s in range(SLOTS):
                    group(i, s)

        @block.scalar
        def _(act):
            act.sem_inc(window_out, 2 * SLOTS)
            act.wait_ge(zeros_ready, 1)
            for j in range(NJ):
                nc.scalar.dma_start(adj_rows[:, j, :], zeros).then_inc(zero_filled, 16)

            def window_rows(g, s, piece):
                k0, k1 = PIECES[piece]
                act.wait_ge(window_made, g * 2 + (piece + 1))
                if piece == 0:
                    nc.scalar.activation(later[s], ps[7][0:P, REP_AT:REP_AT + 2 * G], ACT.Copy).then_inc(repeat_out, 1)
                nc.scalar.activation(msg[s][:, k0:k1, :],
                                     ps[7][0:P, 0:(k1 - k0) * C].rearrange("p (k c) -> p k c", c=C),
                                     ACT.Copy, scale=1.0 / Q_UP).then_inc(window_out, 1)

            def message(g, s):
                act.wait_ge(pre_ready, g + 1)
                nc.scalar.activation(msg[s], msg[s], ACT.Silu).then_inc(msg_done, 1)
                act.wait_ge(msg_done, g + 1)
                nc.scalar.activation(msg16[s][:, :, 0:C], msg[s], ACT.Copy).then_inc(msg_hi_ready, 1)

            window_rows(0, 0, 0)
            window_rows(0, 0, 1)
            with nc.scalar.Fori(0, BODY - 1) as i:
                for s in range(SLOTS):
                    window_rows(i * SLOTS + (s + 1), (s + 1) % SLOTS, 0)
                    message(i * SLOTS + s, s)
                    window_rows(i * SLOTS + (s + 1), (s + 1) % SLOTS, 1)
            for s in range(SLOTS):
                g = (BODY - 1) * SLOTS + s
                if g + 1 < NG:
                    window_rows(g + 1, (s + 1) % SLOTS, 0)
                message(g, s)
                if g + 1 < NG:
                    window_rows(g + 1, (s + 1) % SLOTS, 1)
            act.wait_ge(out0_ready, 1)
            for c, (d0, nd) in enumerate(CHUNKS):
                if c >= 2:
                    act.wait_ge(out0_turned, c - 1)
                nc.scalar.activation(halves_sb[c % 2][:, 0:nd], ps[c][:, 0:nd], ACT.Copy).then_inc(out0_copied, 1)
            act.wait_ge(h1_ready, 1)
            nc.scalar.activation(hh[0][0][:, :, 0:C], norm_c, ACT.Copy, scale=H_UP).then_inc(hi_ready, 1)
            act.wait_ge(hh_ready, NC)
            for k, (c, q, j0, nj) in enumerate(SPLITS):
                nd = CHUNKS[c][1]
                act.wait_ge(adj_loaded[k % 2], 16 * (k // 2 + 1))
                if (c, q) in streamed_of and streamed_of[c, q] >= 2:
                    act.wait_ge(unit_stored, 16 * (streamed_of[c, q] - 1))
                nc.scalar.activation(split_out(c, q)[:, :, 0, :],
                                     stage[k % 2][:, 0:nj * nd].rearrange("p (j d) -> p j d", d=nd),
                                     ACT.Copy, scale=A_HI).then_inc(adj_hi_ready, 1)
                if k >= 1 and SPLITS[k - 1][:2] in streamed_of:
                    v = streamed_of[SPLITS[k - 1][:2]]
                    act.wait_ge(adj_split, k)
                    if v:
                        act.wait_ge(unit_stored, 16 * v)
                    nc.scalar.dma_start(split_d[v], ring[v % 2].rearrange("p j h d -> p (j h d)")
                                        ).then_inc(unit_stored, 16)
            act.wait_ge(unit_stored, 16 * STREAMED)
            act.sem_inc(bank_free, NC)
            with nc.scalar.Fori(0, LAYERS // 2) as i:
                for half in range(2):
                    for c, (d0, nd) in enumerate(CHUNKS):
                        k = i * (2 * NC) + (half * NC + c)
                        b = (half * NC + c) % 2
                        w = nd // P * C
                        act.wait_ge(product_ready, k + 1)
                        nc.scalar.activation(halves_sb[b][:, 0:nd], ps[ACC[c]][:, 0:nd], ACT.Copy,
                                             scale=UNSCALE).then_inc(bank_free, 1)
                        act.wait_ge(turned, k + 1)
                        nc.scalar.activation(square[:, 0:w], ps[TURN[c]][0:P, 0:w], ACT.Square).then_inc(squared, 1)
                        act.wait_ge(eps_ready, k + 1)
                        nc.scalar.activation(n_tanh[b][:, 0:nd // P], n_eps[b][:, 0:nd // P],
                                             ACT.Tanh).then_inc(tanh_ready, 1)
                        act.wait_ge(new_ready, k + 1)
                        nc.scalar.activation(
                            hh[1 - half][0][:, d0 // P:(d0 + nd) // P, 0:C],
                            h_new[:, 0:w].rearrange("p (j c) -> p j c", c=C), ACT.Copy,
                            scale=H_UP).then_inc(hi_ready, 1)

        @block.vector
        def _(dve):
            done = [0]

            def link(ins):
                done[0] += 1
                ins.then_inc(dve_step, 1)
                dve.wait_ge(dve_step, done[0])

            def rsqrt(did, y, t, v):
                yi = y.bitcast(I32)
                did(nc.vector.tensor_scalar(yi, v.bitcast(I32), 1, None, ALU.logical_shift_right))
                did(nc.vector.tensor_scalar(yi, yi, -1.0, RSQRT_MAGIC, ALU.mult, ALU.add))
                for _ in range(3):
                    did(nc.vector.scalar_tensor_tensor(out=t, in0=y, scalar=-0.5, in1=y, op0=ALU.mult, op1=ALU.mult))
                    did(nc.vector.tensor_tensor(t, t, v, ALU.mult))
                    did(nc.vector.scalar_tensor_tensor(out=y, in0=t, scalar=1.5, in1=y, op0=ALU.add, op1=ALU.mult))

            def layernorm_relu(x, out, sq):
                mean, var, neg, rstd = (s[:, :] for s in stat)
                wide = (lambda v: v.unsqueeze(2).to_broadcast([P, NJ, C]))
                link(nc.vector.tensor_reduce(out=mean, in_=x, axis=AX.X, op=ALU.add))
                link(nc.vector.tensor_scalar(neg, mean, -1.0 / C, None, ALU.mult))
                link(nc.vector.tensor_tensor(out, x, wide(neg), ALU.add))
                link(nc.vector.tensor_tensor(sq, out, out, ALU.mult))
                link(nc.vector.tensor_reduce(out=var, in_=sq, axis=AX.X, op=ALU.add))
                link(nc.vector.tensor_scalar(neg, var, 1.0 / C, LN_EPS, ALU.mult, ALU.add))
                rsqrt(link, rstd, mean, neg)
                link(nc.vector.tensor_tensor(sq, out, wide(rstd), ALU.mult))
                return nc.vector.tensor_scalar(out, sq, 0.0, None, ALU.max)

            dve.sem_inc(keyrow_free, SLOTS)
            nc.vector.memset(zeros, 0.0).then_inc(zeros_ready, 1)
            nc.vector.memset(zeros16, 0.0).then_inc(zeros_ready, 1)
            dve.wait_ge(x_loaded, 16)
            layernorm_relu(z_acc[:], norm_c, norm_s).then_inc(h0_ready, 1)
            dve.wait_ge(iotas_ready, 4)
            link(nc.vector.tensor_scalar(ident, iota_sq, 0.0, None, ALU.is_equal))
            nc.vector.memset(ones, 1.0)
            nc.vector.memset(before[:, 0, :], 1.0)
            nc.vector.tensor_scalar(before[:, 1, :], iota_sq, 0.0, None, ALU.is_lt)
            link(nc.vector.tensor_copy(spare_f, spare_i))
            nc.vector.tensor_scalar(row_f, spare_f, -float(N * N), None, ALU.add)
            nc.vector.tensor_scalar(fold_b, iota_fold, -float(C), None, ALU.is_equal)
            link(nc.vector.tensor_scalar(fold[:], iota_fold, 0.0, None, ALU.is_equal))
            link(nc.vector.tensor_tensor(fold[:], fold[:], fold_b, ALU.add))
            dve.sem_inc(ident_ready, 1)
            dve.wait_ge(edges_loaded, 48)
            nc.vector.tensor_copy(dst_row[0:TROWS], dst_row_i[0:TROWS])
            link(nc.vector.tensor_copy(src_row[0:TROWS], src_row_i[0:TROWS]))
            link(nc.vector.scalar_tensor_tensor(
                out=key_row[0:TROWS].rearrange("q a p -> q (a p)"),
                in0=src_row[0:TROWS].rearrange("q a p -> q (a p)"), scalar=float(N),
                in1=dst_row[0:TROWS].rearrange("q a p -> q (a p)"), op0=ALU.mult, op1=ALU.add))
            dve.sem_inc(key_ready, 1)
            for n, column in enumerate((src_f, dst_f, w_up)):
                for half, (a0, a1) in enumerate(((0, 6), (6, G))):
                    dve.wait_ge(rows_turned, 2 * n + half + 1)
                    nc.vector.tensor_copy(column[:, a0 * TROWS:a1 * TROWS],
                                          ps[2 * (n % 2) + half][0:P, 0:(a1 - a0) * TROWS]
                                          ).then_inc(columns_copied, 1)
            dve.wait_ge(columns_copied, 6)
            link(nc.vector.scalar_tensor_tensor(out=key_f, in0=src_f, scalar=float(N), in1=dst_f,
                                                op0=ALU.mult, op1=ALU.add))
            dve.sem_inc(columns_ready, 1)
            link(nc.vector.tensor_scalar(w_up, w_up, W_UP, None, ALU.mult))
            link(nc.vector.tensor_copy(w16[:, :, 0], w_up))
            link(nc.vector.tensor_tensor(w16[:, :, 1], w_up, w16[:, :, 0], ALU.subtract))
            link(nc.vector.tensor_scalar(to_spare, key_f, -1.0, spare_f, ALU.mult, ALU.add))
            second = to_spare.rearrange("p (g k) -> p g k", k=G)[:, :, 1:G:2]
            link(nc.vector.tensor_scalar(second, second, float(P), None, ALU.add))
            dve.wait_ge(firsts_spread, 1)
            link(nc.vector.tensor_scalar(first_node, ps[4][0:P, 0:NG], float(N - WINDOW), None, ALU.min))
            nc.vector.tensor_copy(first_i, first_node)
            nc.vector.tensor_scalar(window_node, first_node, row_f, None, ALU.add)
            grouped = (lambda v: v.rearrange("p (g k) -> p g k", k=G))
            link(nc.vector.tensor_tensor(grouped(cols), grouped(dst_f),
                                         first_node.unsqueeze(2).to_broadcast([P, NG, G]), ALU.subtract))
            link(nc.vector.tensor_scalar(in_window, cols, 0.0, None, ALU.is_ge))
            link(nc.vector.scalar_tensor_tensor(out=in_window, in0=cols, scalar=float(WINDOW), in1=in_window,
                                                op0=ALU.is_lt, op1=ALU.mult))
            link(nc.vector.tensor_scalar(cols, dst_f, -1.0, float(N), ALU.mult, ALU.add))
            link(nc.vector.tensor_tensor(cols, cols, in_window, ALU.mult))
            link(nc.vector.tensor_tensor(q_index, cols, dst_f, ALU.add))
            link(nc.vector.tensor_reduce(out=first_node, in_=grouped(in_window), axis=AX.X, op=ALU.add))
            dve.sem_inc(inside_ready, 1)
            dve.wait_ge(inside_summed, 1)
            link(nc.vector.tensor_scalar(outside, ps[5][0:P, 0:NG], -1.0, float(G * P), ALU.mult, ALU.add))
            dve.sem_inc(windows_ready, 1)
            dve.wait_ge(bn_loaded, 64)
            link(nc.vector.tensor_scalar(bias, bn[:, 3, :], BN_EPS, None, ALU.add))
            rsqrt(link, inv, bn[:, 3, :], bias)
            link(nc.vector.tensor_tensor(inv, inv, bn[:, 0, :], ALU.mult))
            link(nc.vector.tensor_tensor(bias, inv, bn[:, 2, :], ALU.mult))
            link(nc.vector.tensor_tensor(bias, bn[:, 1, :], bias, ALU.subtract))
            dve.wait_ge(w_turned, 1)
            link(nc.vector.tensor_copy(w_t[0:C, :], ps[3][0:C, 0:2 * C]))
            link(nc.vector.tensor_tensor(w_t[0:C, 0:C], w_t[0:C, 0:C], w_t[0:C, C:2 * C], ALU.subtract))
            nc.vector.tensor_tensor(w_fold[0:C, 0:C], w_t[0:C, 0:C], inv[0:C], ALU.mult).then_inc(w_folded, 1)
            nc.vector.tensor_tensor(w_fold[0:C, C:2 * C], w_t[0:C, C:2 * C], inv[0:C], ALU.mult).then_inc(w_folded, 1)
            for c, (d0, nd) in enumerate(CHUNKS):
                dve.wait_ge(h0_turned, c + 1)
                nc.vector.tensor_copy(h0t[0:C, d0:d0 + nd], ps[4 + c % 2][0:C, 0:nd]).then_inc(h0t_copied, 1)
            for c, (d0, nd) in enumerate(CHUNKS):
                dve.wait_ge(pq_made, c + 1)
                nj = nd // P
                got = ps[6 + c % 2][0:P, 0:nj * 2 * C].rearrange("p (j c) -> p j c", c=2 * C)
                nc.vector.tensor_tensor(pq[:, d0 // P:d0 // P + nj, 0:C], got[:, :, 0:C],
                                        bias.unsqueeze(1).to_broadcast([P, nj, C]), ALU.add)
                link(nc.vector.tensor_copy(pq[:, d0 // P:d0 // P + nj, C:2 * C], got[:, :, C:2 * C]))
                dve.sem_inc(pq_copied, 1)
            link(nc.vector.tensor_scalar(q16[:, :, 0:C], pq[:, :, C:2 * C], Q_UP, None, ALU.mult))
            link(nc.vector.scalar_tensor_tensor(out=q16[:, :, C:2 * C], in0=pq[:, :, C:2 * C], scalar=Q_UP,
                                                in1=q16[:, :, 0:C], op0=ALU.mult, op1=ALU.subtract))
            dve.sem_inc(pq_ready, 1)

            STEPS0 = 6
            base0 = done[0]

            def prep(g, slot_turn, s, step0):
                step = [0]

                def did(ins):
                    step[0] += 1
                    ins.then_inc(dve_step, 1)
                    dve.wait_ge(dve_step, step0 + step[0])

                own = bass.ds(g * G, G)
                dve.wait_ge(bundles_begun, g * NB + 1)
                nc.vector.tensor_copy(w16_c[s], w16[:, own, :])
                nc.vector.tensor_copy(src_x[s], src_f[:, own])
                nc.vector.tensor_copy(src_c[s], src_f[:, own])
                nc.vector.tensor_copy(node_c, window_node[:, bass.ds(g, 1)])
                did(nc.vector.tensor_copy(key_c, key_f[:, own]))
                dve.wait_ge(keyrow_loaded[s], slot_turn * 48 + 48)
                at = 0
                for bundle in BUNDLES:
                    for n, k in enumerate(bundle):
                        w = (n + 1) * P
                        nc.vector.scalar_tensor_tensor(
                            out=repeat[s][:, at:at + w],
                            in0=keyrow[s][:, bundle[0]:k + 1, :].rearrange("p a b -> p (a b)"),
                            scalar=key_c[:, k:k + 1],
                            in1=before[:, 1 - n:2, :].rearrange("p a b -> p (a b)"),
                            op0=ALU.is_equal, op1=ALU.mult, accum_out=count[:, k:k + 1])
                        at += w
                did(nc.vector.tensor_scalar(pick_dst[s], dstrow[s], node_c, None, ALU.is_equal))
                dve.sem_inc(keyrow_free, 1)
                dve.sem_inc(repeat_ready, 1)
                did(nc.vector.scalar_tensor_tensor(out=shift, in0=count, scalar=1.0, in1=to_spare[:, own],
                                                   op0=ALU.min, op1=ALU.mult))
                did(nc.vector.tensor_tensor(adj_x[s], shift, key_f[:, own], ALU.add))
                dve.wait_ge(repeat_out, g + 1)
                did(nc.vector.tensor_reduce(out=shift, in_=later[s].rearrange("p (k h) -> p k h", h=2), axis=AX.X, op=ALU.add))
                did(nc.vector.tensor_tensor(w_sum[s], w_up[:, own], shift, ALU.add))
                dve.sem_inc(prep_ready, 1)
                assert step[0] == STEPS0

            def use(g, slot_turn, s, step0):
                dve.wait_ge(gathered[s], slot_turn * (16 * G) + 16 * G)
                dve.wait_ge(q_ready, g + 1)
                dve.wait_ge(window_out, g * 2 + (2 + 2 * SLOTS))
                nc.vector.tensor_tensor(msg[s], p_g[s], msg[s], ALU.add).then_inc(pre_ready, 1)
                for k in range(G):
                    t = g * G + k
                    if k == OH:
                        dve.wait_ge(msg_hi_ready, g + 1)
                        nc.vector.tensor_tensor(msg16[s][:, :, C:2 * C], msg[s], msg16[s][:, :, 0:C],
                                                ALU.subtract).then_inc(msg_ready, 1)
                    dve.wait_ge(onehot_free, t + 1)
                    nc.vector.tensor_scalar(onehot[(s * G + k) % OH], iota16, src_c[s][:, k:k + 1], None,
                                            ALU.is_equal).then_inc(onehot_ready, 1)

            S = STEPS0
            prep(0, 0, 0, base0)
            with nc.vector.Fori(0, BODY - 1) as i:
                for s in range(SLOTS):
                    n = (s + 1) % SLOTS
                    prep(i * SLOTS + (s + 1), i + (s + 1) // SLOTS, n, i * (S * SLOTS) + (base0 + S * (s + 1)))
                    use(i * SLOTS + s, i, s, None)
            for s in range(SLOTS):
                g = (BODY - 1) * SLOTS + s
                if g + 1 < NG:
                    prep(g + 1, (g + 1) // SLOTS, (s + 1) % SLOTS, base0 + S * (g + 1))
                use(g, g // SLOTS, s, None)
            done[0] = base0 + S * NG

            for c, (d0, nd) in enumerate(CHUNKS):
                nj = nd // P
                v = z_acc[:, d0 // P:d0 // P + nj, :]
                dve.wait_ge(out0_turned, c + 1)
                nc.vector.tensor_tensor(v, v, ps[c][0:P, 0:nj * C].rearrange("p (j c) -> p j c", c=C),
                                        ALU.add).then_inc(out0_added, 1)
            dve.wait_ge(out0_added, NC)
            link(layernorm_relu(z_acc[:], norm_c, norm_s))
            dve.sem_inc(h1_ready, 1)
            dve.wait_ge(mix_loaded, 16)
            link(nc.vector.scalar_tensor_tensor(out=z_acc[:], in0=norm_c, scalar=mix[:, 0:1], in1=z_acc[:],
                                                op0=ALU.mult, op1=ALU.add))
            dve.wait_ge(hi_ready, 1)
            link(nc.vector.scalar_tensor_tensor(out=hh[0][0][:, :, C:2 * C], in0=norm_c, scalar=H_UP,
                                                in1=hh[0][0][:, :, 0:C], op0=ALU.mult, op1=ALU.subtract))
            link(nc.vector.tensor_scalar(hh[0][1], hh[0][0], A_HI, None, ALU.mult))
            dve.sem_inc(hh_ready, NC)
            for k, (c, q, j0, nj) in enumerate(SPLITS):
                nd = CHUNKS[c][1]
                dve.wait_ge(adj_hi_ready, k + 1)
                o = split_out(c, q)
                nc.vector.scalar_tensor_tensor(out=o[:, :, 1, :], in0=o[:, :, 0, :], scalar=-1.0 / A_HI,
                                               in1=stage[k % 2][:, 0:nj * nd].rearrange("p (j d) -> p j d", d=nd),
                                               op0=ALU.mult, op1=ALU.add).then_inc(adj_split, 1)
                dve.wait_ge(adj_split, k + 1)
                dve.sem_inc(stage_free, 1)

            base1 = done[0]
            STEPS = 17
            with nc.vector.Fori(0, LAYERS // 2) as i:
                for half in range(2):
                    layer = i * 2 + (half + 1)
                    for c, (d0, nd) in enumerate(CHUNKS):
                        kk = half * NC + c
                        k = i * (2 * NC) + kk
                        b = kk % 2
                        nj = nd // P
                        w = nj * C
                        step = [0]

                        def did(ins):
                            step[0] += 1
                            ins.then_inc(dve_step, 1)
                            dve.wait_ge(dve_step, i * (2 * NC * STEPS) + (base1 + kk * STEPS + step[0]))

                        new = h_new[:, 0:w].rearrange("p (j c) -> p j c", c=C)
                        dve.wait_ge(squared, k + 1)
                        did(nc.vector.tensor_reduce(out=n_sq[b][:, 0:nj],
                                                    in_=square[:, 0:w].rearrange("p (j c) -> p j c", c=C),
                                                    axis=AX.X, op=ALU.add))
                        rsqrt(did, factor[b][:, 0:nj], n_eps[b][:, 0:nj], n_sq[b][:, 0:nj])
                        did(nc.vector.tensor_tensor(n_tanh[b][:, 0:nj], factor[b][:, 0:nj], n_sq[b][:, 0:nj],
                                                    ALU.mult))
                        nc.vector.tensor_scalar(n_eps[b][:, 0:nj], n_tanh[b][:, 0:nj], NORM_EPS, None,
                                                ALU.add).then_inc(eps_ready, 1)
                        dve.wait_ge(eps_ready, k + 1)
                        did(nc.vector.reciprocal(n_sq[b][:, 0:nj], n_eps[b][:, 0:nj]))
                        dve.wait_ge(tanh_ready, k + 1)
                        did(nc.vector.tensor_tensor(factor[b][:, 0:nj], n_tanh[b][:, 0:nj], n_sq[b][:, 0:nj],
                                                    ALU.mult))
                        nc.vector.tensor_tensor(new, ps[TURN[c]][0:P, 0:w].rearrange("p (j c) -> p j c", c=C),
                                                factor[b][:, 0:nj].unsqueeze(2).to_broadcast([P, nj, C]),
                                                ALU.mult).then_inc(new_ready, 1)
                        dve.wait_ge(new_ready, k + 1)
                        zc = z_acc[:, d0 // P:d0 // P + nj, :]
                        nc.vector.scalar_tensor_tensor(out=zc, in0=new, scalar=mix[:, bass.ds(layer, 1)], in1=zc,
                                                       op0=ALU.mult, op1=ALU.add)
                        dve.wait_ge(hi_ready, k + 2)
                        hi = hh[1 - half][0][:, d0 // P:d0 // P + nj, :]
                        did(nc.vector.scalar_tensor_tensor(out=hi[:, :, C:2 * C], in0=new, scalar=H_UP,
                                                           in1=hi[:, :, 0:C], op0=ALU.mult, op1=ALU.subtract))
                        did(nc.vector.tensor_scalar(hh[1 - half][1][:, d0 // P:d0 // P + nj, :], hi, A_HI, None,
                                                    ALU.mult))
                        dve.sem_inc(hh_ready, 1)
                        assert step[0] == STEPS

        @block.tensor
        def _(pe):
            pe.wait_ge(ident_ready, 1)
            pe.wait_ge(key_ready, 1)
            for n, row in enumerate((src_row, dst_row, w_row)):
                for half, (a0, a1) in enumerate(((0, 6), (6, G))):
                    if n == 2:
                        pe.wait_ge(columns_copied, half + 1)
                    for a in range(a0, a1):
                        last = nc.tensor.transpose(ps[2 * (n % 2) + half][0:P, (a - a0) * TROWS:(a - a0 + 1) * TROWS],
                                                   row[0:TROWS, a, :], ident[0:TROWS, 0:TROWS])
                    last.then_inc(rows_turned, 1)
            pe.wait_ge(columns_ready, 1)
            nc.tensor.matmul(ps[4][0:P, 0:NG], ones[0:1, :], dst_f[0:1, 0:T:G], start=True,
                             stop=True).then_inc(firsts_spread, 1)
            pe.wait_ge(inside_ready, 1)
            nc.tensor.matmul(ps[5][0:P, 0:NG], ones, first_node, start=True, stop=True).then_inc(inside_summed, 1)
            pe.wait_ge(windows_ready, 1)
            pe.wait_ge(w_loaded, 16)
            for h in range(2):
                last = nc.tensor.transpose(ps[3][0:C, h * C:(h + 1) * C], w_nat[0:C, h * C:(h + 1) * C],
                                           ident[0:C, 0:C])
            last.then_inc(w_turned, 1)
            pe.wait_ge(h0_ready, 1)
            for c, (d0, nd) in enumerate(CHUNKS):
                if c >= 2:
                    pe.wait_ge(h0t_copied, c - 1)
                for u in range(nd // P):
                    last = nc.tensor.transpose(ps[4 + c % 2][0:C, u * P:(u + 1) * P], norm_c[:, d0 // P + u, :], ident)
                last.then_inc(h0_turned, 1)
            pe.wait_ge(w_folded, 2)
            pe.wait_ge(h0t_copied, NC)
            for c, (d0, nd) in enumerate(CHUNKS):
                if c >= 2:
                    pe.wait_ge(pq_copied, c - 1)
                for u in range(nd // P):
                    last = nc.tensor.matmul(ps[6 + c % 2][0:P, u * 2 * C:(u + 1) * 2 * C],
                                            h0t[0:C, d0 + u * P:d0 + (u + 1) * P], w_fold[0:C, :],
                                            start=True, stop=True)
                last.then_inc(pq_made, 1)

            pe.wait_ge(zeros_ready, 2)
            pe.wait_ge(pq_ready, 1)
            for c, (d0, nd) in enumerate(CHUNKS):
                nc.tensor.matmul(ps[c][:, 0:nd], zeros16[:, 0:128], zeros16[:, 128:128 + nd], start=True, stop=False)
            pe.sem_inc(onehot_free, OH)

            def sum_repeats(g, s):
                pe.wait_ge(repeat_ready, g + 1)
                at = 0
                for bundle in BUNDLES:
                    starts = []
                    for n in range(len(bundle)):
                        starts.append(at)
                        at += (n + 1) * P
                    for m, k in enumerate(bundle):
                        for n in range(m, len(bundle)):
                            nc.tensor.matmul(
                                ps[7][0:P, REP_AT + 2 * k:REP_AT + 2 * k + 2],
                                repeat[s][:, starts[n] + m * P:starts[n] + (m + 1) * P],
                                w16_c[s][:, bundle[n], :], start=(n == m), stop=(n == len(bundle) - 1))

            def window_rows(g, s, piece):
                k0, k1 = PIECES[piece]
                for k in range(k0, k1):
                    for h in range(2):
                        last = nc.tensor.matmul(ps[7][0:P, (k - k0) * C:(k - k0 + 1) * C], pick_dst[s][0:WINDOW, k, :],
                                                q_window[s][0:WINDOW, h * C:(h + 1) * C], start=(h == 0), stop=(h == 1))
                last.then_inc(window_made, 1)

            def second_piece(g, s):
                pe.wait_ge(window_out, g * 2 + (1 + 2 * SLOTS))
                window_rows(g, s, 1)

            def add_messages(g, s, tiles):
                pe.wait_ge(msg_ready, g + 1)
                for k in tiles:
                    pe.wait_ge(onehot_ready, g * G + (k + 1))
                    for c, (d0, nd) in enumerate(CHUNKS):
                        last = nc.tensor.matmul(ps[c][:, 0:nd], msg16[s][:, k, :],
                                                onehot[(s * G + k) % OH][:, d0:d0 + nd], start=False, stop=False)
                    last.then_inc(onehot_free, 1)

            def group(g, s, last_group):
                n = (s + 1) % SLOTS
                if not last_group:
                    pe.wait_ge(window_out, g * 2 + (2 + 2 * SLOTS))
                    sum_repeats(g + 1, n)
                    window_rows(g + 1, n, 0)
                add_messages(g, s, range(0, 6))
                if not last_group:
                    second_piece(g + 1, n)
                add_messages(g, s, range(6, G))

            sum_repeats(0, 0)
            window_rows(0, 0, 0)
            second_piece(0, 0)
            with nc.tensor.Fori(0, BODY - 1) as i:
                for s in range(SLOTS):
                    group(i * SLOTS + s, s, False)
            for s in range(SLOTS):
                g = (BODY - 1) * SLOTS + s
                group(g, s, g + 1 == NG)
            for c, (d0, nd) in enumerate(CHUNKS):
                last = nc.tensor.matmul(ps[c][:, 0:nd], zeros16[:, 0:128], zeros16[:, 128:128 + nd],
                                        start=False, stop=True)
            last.then_inc(out0_ready, 1)
            for c, (d0, nd) in enumerate(CHUNKS):
                pe.wait_ge(out0_copied, c + 1)
                for u in range(nd // P):
                    last = nc.tensor.matmul(ps[c][0:P, u * C:(u + 1) * C], halves_sb[c % 2][:, u * P:(u + 1) * P],
                                            fold[:], start=True, stop=True)
                last.then_inc(out0_turned, 1)

            pe.sem_inc(unit_used, RING)
            pe.wait_ge(adj_split, len(SPLITS))

            def turn(c, k, b):
                pe.wait_ge(bank_free, k + (NC + 1))
                for u in range(CHUNKS[c][1] // P):
                    last = nc.tensor.matmul(ps[TURN[c]][0:P, u * C:(u + 1) * C], halves_sb[b][:, u * P:(u + 1) * P],
                                            fold[:], start=True, stop=True)
                last.then_inc(turned, 1)

            with nc.tensor.Fori(0, LAYERS // 2) as i:
                for half in range(2):
                    for c, (d0, nd) in enumerate(CHUNKS):
                        kk = half * NC + c
                        k = i * (2 * NC) + kk
                        pe.wait_ge(bank_free, k + (NC + 1 - (3 if 3 <= c < NC - 1 else 4 if c < 3 else NC)))
                        for j in range(NJ):
                            if c == 0 and j % BPC == 0:
                                pe.wait_ge(hh_ready, i * (2 * NC) + (half * NC + j // BPC + 1))
                            q, jj = j // UJ, j % UJ
                            if c == NC - 1:
                                q, a = 0, last_adj[:, j]
                            elif (c, q) in resident_of:
                                a = res[resident_of[c, q]][:, jj]
                            else:
                                v = half * STREAMED + streamed_of[c, q]
                                a = ring[v % RING][:, jj]
                                if jj == 0:
                                    pe.wait_ge(streamed[v % RING],
                                               i * (2 * STREAMED // RING * 16) + 16 * (v // RING + 1))
                            for part in range(2):
                                last = nc.tensor.matmul(ps[ACC[c]][:, 0:nd], hh[half][part][:, j, :], a[:, part, :],
                                                        start=(j == 0 and part == 0),
                                                        stop=(j == NJ - 1 and part == 1))
                            if (c, q) in streamed_of and jj == UJ - 1:
                                last.then_inc(unit_used, 1)
                            if j == 12 and c > 0:
                                turn(c - 1, k - 1, (kk - 1) % 2)
                        last.then_inc(product_ready, 1)
                    turn(NC - 1, k, kk % 2)


REP_AT = 400
ACC = [0, 1, 2, 0, 1, 2, 3]
TURN = [4, 5, 6, 4, 5, 6, 7]


_INS = ['x', 'src', 'dst', 'edge_weight', 'L0_gnn_W', 'L0_gnn_bn_gamma', 'L0_gnn_bn_beta', 'L0_gnn_bn_mean',
        'L0_gnn_bn_var', 'L1_gnn_manifold_weights']


def kernel(**inputs):
    import numpy as _np
    import concourse.bacc as _bacc
    from concourse import mybir as _mybir
    from concourse.bass_utils import run_bass_kernel_spmd as _run

    nc = _bacc.Bacc("TRN2", target_bir_lowering=False, num_devices=1)
    arrays, args = {}, []
    for name in _INS:
        a = _np.ascontiguousarray(inputs[name])
        arrays[f"in_{name}_dram"] = a
        args.append(nc.dram_tensor(f"in_{name}_dram", a.shape, _mybir.dt.from_np(a.dtype), kind="ExternalInput").ap())
    args.append(nc.dram_tensor("out_0_dram", (N, C), _mybir.dt.float32, kind="ExternalOutput").ap())
    gnn_kernel(nc, *args)
    r = _run(nc, [arrays], core_ids=[0])
    return r.results[0]["out_0_dram"]
```

```python
from contextlib import ExitStack

import concourse.bass as bass
from concourse import mybir

F32 = mybir.dt.float32
F16 = mybir.dt.float16
I32 = mybir.dt.int32
I16 = mybir.dt.int16
ALU = mybir.AluOpType
ACT = mybir.ActivationFunctionType
AX = mybir.AxisListType

N = 3125
C = 64
P = 125
NJ = N // P
E = 103125
T = E // P
G = 11
SLOTS = 3
NG = T // G
BODY = NG // SLOTS
OH = 3
WIDE = 4
BUNDLES = [tuple(range(k, min(k + WIDE, G))) for k in range(0, G, WIDE)]
NB = len(BUNDLES)
PIECES = [(0, 6), (6, G)]
WINDOW = P
TROWS = T // G
Q_UP = 256.0
CHUNK = 500
BPC = CHUNK // P
CHUNKS = [(c * CHUNK, min(CHUNK, N - c * CHUNK)) for c in range(-(-N // CHUNK))]
NC = len(CHUNKS)
LAYERS = 10
UJ = 5
NQ = NJ // UJ
RESIDENT = (1, 4)
STREAMED = (NC - 1) * (NQ - len(RESIDENT))
RING = 3
STAGES = 10
LN_EPS = 1e-5
BN_EPS = 1e-5
NORM_EPS = 1e-8
W_UP = 512.0
RSQRT_MAGIC = float(0x5F3759DF)
A_HI = 2.0 ** -11
H_UP = 4096.0
UNSCALE = 1.0 / (W_UP * A_HI * H_UP)


def gnn_kernel(nc, x_d, src_d, dst_d, ew_d, w_d, gamma_d, beta_d, mean_d, var_d, mix_d, out_d):
    p_d = nc.dram_tensor("p_rows", (N, C), F32, kind="Internal").ap()
    q_d = nc.dram_tensor("q_rows", (N + 1, C), F32, kind="Internal").ap()
    q16_d = nc.dram_tensor("q_halves", (N, 2 * C), F16, kind="Internal").ap()
    key_d = nc.dram_tensor("key_rows", (T, P), F32, kind="Internal").ap()
    adj_d = nc.dram_tensor("adjacency", (N * N + WIDE * P, 1), F32, kind="Internal").ap()
    adj_rows = adj_d[0:N * N, :].rearrange("(j p d) o -> p j (d o)", p=P, d=N)
    split_d = nc.dram_tensor("split_units", (STREAMED, P, UJ * 2 * CHUNK), F16, kind="Internal").ap()

    ctx = ExitStack()
    with ctx:
        def sb(name, shape, dt):
            return ctx.enter_context(nc.sbuf_tensor(name, shape, dt))

        def sem(name):
            return ctx.enter_context(nc.semaphore(name))

        ps = [ctx.enter_context(nc.psum_tensor(f"bank{b}", [128, 512], F32)) for b in range(8)]

        z_acc = sb("z_acc", [P, NJ, C], F32)
        mix = sb("mix", [P, LAYERS + 1], F32)
        fold = sb("fold", [128, C], F32)
        hh_all = sb("hh_all", [P, 4, NJ, 2 * C], F16)
        hh = [[hh_all[:, 2 * a + s] for s in range(2)] for a in range(2)]
        stage0 = sb("stage0", [P, UJ * CHUNK], F32)
        UNIT = UJ * 2 * CHUNK
        LAST = NJ * 2 * P
        n_res = (NC - 1) * len(RESIDENT)
        ARENA = (n_res + RING) * UNIT + LAST
        arena = sb("arena", [P, ARENA], F16)
        res = [arena[:, k * UNIT:(k + 1) * UNIT].rearrange("p (j h d) -> p j h d", j=UJ, h=2) for k in range(n_res)]
        last_adj = arena[:, n_res * UNIT:n_res * UNIT + LAST].rearrange("p (j h d) -> p j h d", j=NJ, h=2)
        ring = [arena[:, n_res * UNIT + LAST + k * UNIT:n_res * UNIT + LAST + (k + 1) * UNIT]
                .rearrange("p (j h d) -> p j h d", j=UJ, h=2) for k in range(RING)]
        stage = [stage0[:, :]] + [arena[:, a0:a0 + UNIT].bitcast(F32)
                                  for a0 in range(n_res * UNIT, (n_res + 1 - (STAGES - 1)) * UNIT, -UNIT)]
        at = [0]

        def carve(shape, dt):
            n = 1
            for s in shape:
                n *= s
            halves = n if dt in (F16, I16) else 2 * n
            at[0] += at[0] % 2
            v = arena[:, at[0]:at[0] + halves]
            at[0] += halves
            assert at[0] <= ARENA
            v = v if dt == F16 else v.bitcast(dt)
            if len(shape) == 2:
                v = v.rearrange("p (a b) -> p a b", b=shape[1])
            return v

        src_f = carve([T], F32)
        dst_f = carve([T], F32)
        w_up = carve([T], F32)
        key_f = carve([T], F32)
        to_spare = carve([T], F32)
        in_window = carve([T], F32)
        cols = carve([T], F32)
        q_index = carve([T], I32)
        w16 = carve([T, 2], F16)
        window_node = carve([NG], F32)
        first_node = carve([NG], F32)
        first_i = carve([NG], I32)
        outside = carve([1], I32)
        inside = carve([1], F32)
        beyond = carve([1], I32)
        last_first = carve([1], F32)
        iota16 = carve([N + 1], I16)
        onehot = [carve([N + 1], F16) for _ in range(OH)]
        ident = carve([P], F32)
        ones = carve([P], F32)
        before = carve([WIDE, P], F16)
        iota_sq = carve([P], I32)
        spare_i = carve([1], I32)
        spare_f = carve([1], F32)
        row_f = carve([1], F32)
        rows_at = at[0]
        keyrow = [carve([G, P], F32) for _ in range(SLOTS)]
        dstrow = [carve([G, P], I32) for _ in range(SLOTS)]
        rows = [arena[:, rows_at + k * 2 * G * P:rows_at + (k + 1) * 2 * G * P].bitcast(F32)
                .rearrange("p (a b) -> p a b", b=P) for k in range(6)]
        src_row_i, dst_row_i, w_row, src_row, dst_row, key_row = rows
        src_row_i, dst_row_i = src_row_i.bitcast(I32), dst_row_i.bitcast(I32)
        pick_dst = [carve([G, P], F16) for _ in range(SLOTS)]
        REP = sum(len(b) * (len(b) + 1) // 2 * P for b in BUNDLES)
        repeat = carve([REP], F16)
        count = [carve([G], F32) for _ in range(SLOTS)]
        shift = carve([G], F32)
        src_x = [carve([G], I32) for _ in range(SLOTS)]
        q_x = carve([G], I32)
        adj_x = [carve([G], I32) for _ in range(SLOTS)]
        src_c = [carve([G], F32) for _ in range(SLOTS)]
        key_c = carve([G], F32)
        node_c = carve([1], F32)
        w16_c = [carve([G, 2], F16) for _ in range(SLOTS)]
        later = [carve([2 * G], F32) for _ in range(SLOTS)]
        w_sum = [carve([G], F32) for _ in range(SLOTS)]
        q_window = [carve([2 * C], F16) for _ in range(SLOTS)]
        gathers_at = at[0]
        p_g = [carve([G, C], F32) for _ in range(SLOTS)]
        msg = [carve([G, C], F32) for _ in range(SLOTS)]
        norm_s, norm_c = (hh_all[:, k].rearrange("p j c -> p (j c)").bitcast(F32).rearrange("p (j c) -> p j c", c=C)
                          for k in (2, 3))
        h0t = arena[:, gathers_at:gathers_at + 2 * N].bitcast(F32)
        assert at[0] >= gathers_at + 2 * N
        msg16 = [carve([G, 2 * C], F16) for _ in range(SLOTS)]
        zeros = carve([N], F32)
        zeros16 = carve([128 + CHUNK], F16)
        pq = hh_all[:, 0:2].rearrange("p a j c -> p (a j c)").bitcast(F32).rearrange("p (j c) -> p j c", c=2 * C)
        q16 = hh_all[:, 2]
        w_nat = carve([2 * C], F32)
        w_t = carve([2 * C], F32)
        w_fold = carve([2 * C], F32)
        bn = carve([4, C], F32)
        inv = carve([C], F32)
        bias = carve([C], F32)
        halves_sb = [sb(f"halves_sb{k}", [128, CHUNK], F32) for k in range(2)]
        stat = [sb(f"stat{k}", [P, NJ], F32) for k in range(4)]
        square = sb("square", [P, BPC * C], F32)
        h_new = sb("h_new", [P, BPC * C], F32)
        n_sq = [sb(f"n_sq{k}", [P, BPC], F32) for k in range(2)]
        n_eps = [sb(f"n_eps{k}", [P, BPC], F32) for k in range(2)]
        n_tanh = [sb(f"n_tanh{k}", [P, BPC], F32) for k in range(2)]
        factor = [sb(f"factor{k}", [P, BPC], F32) for k in range(2)]
        iota_fold = halves_sb[1][:, 0:C].bitcast(I32)
        fold_b = halves_sb[0][:, 0:C]

        edges_loaded, x_loaded, bn_loaded, mix_loaded, w_loaded = (
            sem(n) for n in ("edges_loaded", "x_loaded", "bn_loaded", "mix_loaded", "w_loaded"))
        iotas_ready, ident_ready, zeros_ready = sem("iotas_ready"), sem("ident_ready"), sem("zeros_ready")
        first_zeros, other_zeros = sem("first_zeros"), [sem(f"other_zeros{k}") for k in range(2)]
        OTHERS = NQ * (NC - 2) + 1
        THROTTLED = 13
        key_ready, rows_turned, columns_copied, columns_ready, key_stored = (
            sem(n) for n in ("key_ready", "rows_turned", "columns_copied", "columns_ready", "key_stored"))
        firsts_ready, firsts_spread, inside_ready, inside_summed, windows_ready = (
            sem(n) for n in ("firsts_ready", "firsts_spread", "inside_ready", "inside_summed", "windows_ready"))
        window_made, window_out = sem("window_made"), sem("window_out")
        q_ready, q_step, q_landed = sem("q_ready"), sem("q_step"), sem("q_landed")
        h0_ready, h0_turned, h0t_copied = sem("h0_ready"), sem("h0_turned"), sem("h0t_copied")
        w_turned, w_folded, pq_made, pq_ready, pq_stored = (
            sem("w_turned"), sem("w_folded"), sem("pq_made"), sem("pq_ready"), sem("pq_stored"))
        dve_step = sem("dve_step")
        keyrow_loaded = [sem(f"keyrow_loaded{s}") for s in range(SLOTS)]
        gathered = [sem(f"gathered{s}") for s in range(SLOTS)]
        keyrow_free, bundles_begun, groups_begun, repeat_ready, repeat_out, prep_ready = (
            sem("keyrow_free"), sem("bundles_begun"), sem("groups_begun"), sem("repeat_ready"), sem("repeat_out"), sem("prep_ready"))
        scattered = sem("scattered")
        pre_ready, msg_hi_ready, msg_ready = sem("pre_ready"), sem("msg_hi_ready"), sem("msg_ready")
        msg_done = sem("msg_done")
        pq_copied = sem("pq_copied")
        onehot_ready, onehot_free = sem("onehot_ready"), sem("onehot_free")
        out0_ready, out0_copied, out0_turned, out0_added = (
            sem("out0_ready"), sem("out0_copied"), sem("out0_turned"), sem("out0_added"))
        h1_ready = sem("h1_ready")
        adj_loaded = [sem(f"adj_loaded{k}") for k in range(len(stage))]
        adj_hi_ready, adj_split, stage_free = sem("adj_hi_ready"), sem("adj_split"), sem("stage_free")
        unit_stored = [sem(f"unit_stored{k}") for k in range(RING)]
        streamed = [sem(f"streamed{k}") for k in range(RING)]
        unit_used = sem("unit_used")
        product_ready, bank_free, turned, squared, eps_ready, tanh_ready, new_ready, hi_ready, hh_ready = (
            sem(n) for n in ("product_ready", "bank_free", "turned", "squared", "eps_ready", "tanh_ready",
                             "new_ready", "hi_ready", "hh_ready"))
        out_stored = sem("out_stored")

        block = ctx.enter_context(nc.Block())

        units = [(c, q) for c in range(NC - 1) for q in range(NQ)]
        streamed_of = {}
        resident_of = {}
        for c, q in units:
            if q in RESIDENT:
                resident_of[c, q] = len(resident_of)
            else:
                streamed_of[c, q] = len(streamed_of)

        SPLITS = [(c, q, UJ * q, UJ) for c, q in units] + [(NC - 1, 0, 0, 20), (NC - 1, 1, 20, 5)]

        TAKEN = [len(SPLITS) + 2, len(SPLITS) - 2] + [
            units.index((NC - 2 - k // len(RESIDENT), RESIDENT[-1 - k % len(RESIDENT)]))
            for k in range(len(stage) - 2)]
        STAGE = []
        for k in range(len(SPLITS)):
            STAGE.append(max((s for s in range(len(stage)) if TAKEN[s] > k),
                             key=lambda s: (STAGE[::-1] + [s]).index(s)))

        def split_out(c, q):
            if c == NC - 1:
                return last_adj[:, 20 * q:20 + 5 * q]
            return res[resident_of[c, q]] if (c, q) in resident_of else ring[streamed_of[c, q] % RING]

        @block.sync
        def _(sp):
            sp.dma_start(z_acc[:], x_d.rearrange("(j p) c -> p j c", p=P)).then_inc(x_loaded, 16)
            for dram, tile in ((src_d, src_row_i), (dst_d, dst_row_i), (ew_d, w_row)):
                sp.dma_start(tile[0:TROWS], dram.rearrange("(a q p) -> q a p", q=TROWS, p=P)
                             ).then_inc(edges_loaded, 16)
            sp.dma_start(w_nat[0:C, :], w_d).then_inc(w_loaded, 16)
            for k, dram in enumerate((gamma_d, beta_d, mean_d, var_d)):
                sp.dma_start(bn[:, k, :], dram.partition_broadcast(P)).then_inc(bn_loaded, 16)
            sp.dma_start(mix[:], mix_d.partition_broadcast(P)).then_inc(mix_loaded, 16)
            sp.wait_ge(key_ready, 1)
            sp.dma_start(key_d.rearrange("(a q) p -> q a p", q=TROWS), key_row[0:TROWS]).then_inc(key_stored, 16)
            sp.wait_ge(pq_ready, 1)
            sp.dma_start(p_d.rearrange("(j p) c -> p j c", p=P), pq[:, :, 0:C]).then_inc(pq_stored, 16)
            sp.dma_start(q_d[0:N, :].rearrange("(j p) c -> p j c", p=P), pq[:, :, C:2 * C]).then_inc(pq_stored, 16)
            sp.wait_ge(zeros_ready, 1)
            sp.dma_start(q_d[N:N + 1, :], zeros[0:1, 0:C]).then_inc(pq_stored, 16)
            sp.dma_start(q16_d.rearrange("(j p) c -> p j c", p=P), q16).then_inc(pq_stored, 16)
            sp.wait_ge(pq_stored, 64)
            sp.wait_ge(key_stored, 16)
            sp.wait_ge(columns_ready, 1)
            sp.wait_ge(windows_ready, 1)
            key_flat = key_d.rearrange("t p -> (t p)")
            with sp.Fori(0, BODY) as i:
                for s in range(SLOTS):
                    g = i * SLOTS + s
                    node = sp.value_load(first_i[0:1, bass.ds(g, 1)], min_val=0, max_val=N - WINDOW)
                    sp.wait_ge(keyrow_free, g + 1)
                    for p0, p1 in PARTS:
                        sp.dma_start(keyrow[s][p0:p1].rearrange("p a b -> p (a b)"),
                                     key_flat[bass.ds(g * (G * P), G * P)].partition_broadcast(p1 - p0)
                                     ).then_inc(keyrow_loaded[s], 16)
                        sp.dma_start(dstrow[s][p0:p1].rearrange("p a b -> p (a b)"),
                                     dst_d[bass.ds(g * (G * P), G * P)].partition_broadcast(p1 - p0)
                                     ).then_inc(keyrow_loaded[s], 16)
                    sp.wait_ge(window_out, g * 2 + 2)
                    sp.dma_start(q_window[s][0:WINDOW, :], q16_d[bass.ds(node, WINDOW), :]).then_inc(keyrow_loaded[s], 16)
            sp.wait_ge(scattered, 16 * T + 16)
            for k, (c, q, j0, nj) in enumerate(SPLITS):
                d0, nd = CHUNKS[c]
                if k == 1:
                    sp.wait_ge(out0_ready, 1)
                if STAGE[k] in STAGE[:k]:
                    sp.wait_ge(stage_free, max(m for m in range(k) if STAGE[m] == STAGE[k]) + 1)
                for p0, p1 in PARTS:
                    sp.dma_start(stage[STAGE[k]][p0:p1, 0:nj * nd].rearrange("p (j d) -> p j d", d=nd),
                                 adj_rows[p0:p1, j0:j0 + nj, d0:d0 + nd]).then_inc(adj_loaded[STAGE[k]], 16)
            for k in range(RING):
                sp.wait_ge(unit_stored[k], 32 * (STREAMED // RING))
            sp.wait_ge(unit_used, RING + STREAMED)

            def stream(i, r0):
                for v in range(STREAMED):
                    sp.wait_ge(unit_used, i * (2 * STREAMED) + (r0 * STREAMED + v + 1))
                    for p0, p1 in PARTS:
                        sp.dma_start(ring[v % RING][p0:p1].rearrange("p j h d -> p (j h d)"),
                                     split_d[v, p0:p1]).then_inc(streamed[v % RING], 16)

            stream(0, 1)
            with sp.Fori(0, LAYERS // 2 - 1) as i:
                stream(i, 2)
                stream(i, 3)
            sp.wait_ge(hh_ready, NC * (LAYERS + 1))
            sp.dma_start(out_d.rearrange("(j p) c -> p j c", p=P), z_acc[:]).then_inc(out_stored, 16)
            sp.wait_ge(out_stored, 16)

        @block.gpsimd
        def _(pool):
            nc.gpsimd.iota(iota16, pattern=[[1, N + 1]], base=0, channel_multiplier=0).then_inc(iotas_ready, 1)
            nc.gpsimd.iota(iota_sq, pattern=[[1, P]], base=0, channel_multiplier=-1).then_inc(iotas_ready, 1)
            nc.gpsimd.iota(spare_i, pattern=[[1, 1]], base=N * N, channel_multiplier=1).then_inc(iotas_ready, 1)
            nc.gpsimd.iota(iota_fold, pattern=[[1, C]], base=0, channel_multiplier=-1).then_inc(iotas_ready, 1)
            pool.sem_inc(bundles_begun, 2 * NB)
            pool.wait_ge(zeros_ready, 1)
            nc.gpsimd.dma_start(adj_d[N * N:N * N + WIDE * P, :].rearrange("(p a) o -> p (a o)", a=WIDE), zeros[:, 0:WIDE]
                                ).then_inc(scattered, 16)
            pool.wait_ge(pq_stored, 64)
            pool.wait_ge(windows_ready, 1)

            some_outside = pool.value_load(outside[0:1, 0:1], min_val=0, max_val=E)
            some_beyond = pool.value_load(beyond[0:1, 0:1], min_val=0, max_val=E + N)
            pool.wait_ge(first_zeros, 32 * NQ)
            with pool.If(some_beyond > 0):
                pool.wait_ge(other_zeros[0], 32 * (OTHERS - OTHERS // 2))
                pool.wait_ge(other_zeros[1], 32 * (OTHERS // 2))

            def group(i, s):
                pool.wait_ge(prep_ready, i * SLOTS + (s + 1))
                pool.sem_inc(groups_begun, 1)
                for bundle in BUNDLES:
                    for k in bundle:
                        nc.gpsimd.indirect_dma_start(
                            out=p_g[s][:, k, :], out_offset=None, in_=p_d,
                            in_offset=bass.IndirectOffsetOnAxis(ap=src_x[s][:, k:k + 1], axis=0)
                        ).then_inc(gathered[s], 16)
                    pool.wait_ge(scattered, i * (SLOTS * G * 16) + (s * G + bundle[0]) * 16 + 16)
                    pool.sem_inc(bundles_begun, 1)
                    for k in bundle:
                        nc.gpsimd.indirect_dma_start(
                            out=adj_d, out_offset=bass.IndirectOffsetOnAxis(ap=adj_x[s][:, k:k + 1], axis=0),
                            in_=w_sum[s][:, k:k + 1], in_offset=None, compute_op=ALU.add).then_inc(scattered, 16)
                g = i * SLOTS + s
                with pool.If(some_outside > 0):
                    nc.gpsimd.tensor_copy(q_x, q_index[:, bass.ds(g * G, G)]).then_inc(q_step, 1)
                    pool.wait_ge(q_step, g + 1)
                    pool.wait_ge(gathered[s], i * (16 * G) + 16 * G)
                    pool.sem_inc(groups_begun, 1)
                    for k in range(G):
                        nc.gpsimd.indirect_dma_start(
                            out=p_g[s][:, k, :], out_offset=None, in_=q_d,
                            in_offset=bass.IndirectOffsetOnAxis(ap=q_x[:, k:k + 1], axis=0),
                            compute_op=ALU.add).then_inc(q_landed, 16)
                    pool.wait_ge(q_landed, g * (16 * G) + 16 * G)
                pool.sem_inc(q_ready, 1)

            with nc.gpsimd.Fori(0, BODY) as i:
                for s in range(SLOTS):
                    group(i, s)
                pool.wait_ge(other_zeros[0], 32 * (OTHERS - OTHERS // 2))
                pool.wait_ge(other_zeros[1], 32 * (OTHERS // 2))

        @block.scalar
        def _(act):
            act.sem_inc(window_out, 2 * SLOTS)

            def window_rows(g, s, piece):
                k0, k1 = PIECES[piece]
                act.wait_ge(window_made, g * 2 + (piece + 1))
                if piece == 0:
                    nc.scalar.activation(later[s], ps[7][0:P, REP_AT:REP_AT + 2 * G], ACT.Copy).then_inc(repeat_out, 1)
                nc.scalar.activation(msg[s][:, k0:k1, :],
                                     ps[7][0:P, 0:(k1 - k0) * C].rearrange("p (k c) -> p k c", c=C),
                                     ACT.Copy, scale=1.0 / Q_UP).then_inc(window_out, 1)

            def message(g, s):
                act.wait_ge(pre_ready, g + 1)
                nc.scalar.activation(msg[s], msg[s], ACT.Silu).then_inc(msg_done, 1)
                act.wait_ge(msg_done, g + 1)
                nc.scalar.activation(msg16[s][:, :, 0:C], msg[s], ACT.Copy).then_inc(msg_hi_ready, 1)

            act.wait_ge(zeros_ready, 1)

            def fill(n):
                c, q = n // NQ + 1, n % NQ
                d0, nd = CHUNKS[c]
                j0, nj = (UJ * q, UJ) if c < NC - 1 else (0, NJ)
                if n >= THROTTLED:
                    act.wait_ge(other_zeros[n % 2], 32 * (n // 2))
                for p0, p1 in PARTS:
                    nc.scalar.dma_start(adj_rows[p0:p1, j0:j0 + nj, d0:d0 + nd],
                                        zeros[p0:p1, 0:nj * nd].rearrange("p (j d) -> p j d", d=nd)
                                        ).then_inc(first_zeros if n < 0 else other_zeros[n % 2], 16)

            for n in range(-NQ, 10):
                fill(n)
            act.wait_ge(keyrow_loaded[1], 80)
            for n in range(10, 13):
                fill(n)
            for g, rest in ((0, (13, 16)), (1, (16, 18))):
                window_rows(g, g, 0)
                window_rows(g, g, 1)
                for n in range(*rest):
                    fill(n)
            act.wait_ge(windows_ready, 1)
            some_beyond = act.value_load(beyond[0:1, 0:1], min_val=0, max_val=E + N)
            with act.If(some_beyond > 0):
                for n in range(18, OTHERS):
                    fill(n)
            message(0, 0)
            with act.If(some_beyond < 1):
                for n in range(18, 22):
                    fill(n)
            window_rows(2, 2, 0)
            window_rows(2, 2, 1)
            with act.If(some_beyond < 1):
                for n in range(22, OTHERS):
                    fill(n)
            for g in range(1, SLOTS):
                message(g, g)
                window_rows(g + 2, (g + 2) % SLOTS, 0)
                window_rows(g + 2, (g + 2) % SLOTS, 1)
            with nc.scalar.Fori(1, BODY - 1) as i:
                for s in range(SLOTS):
                    message(i * SLOTS + s, s)
                    window_rows(i * SLOTS + (s + 2), (s + 2) % SLOTS, 0)
                    window_rows(i * SLOTS + (s + 2), (s + 2) % SLOTS, 1)
            for s in range(SLOTS):
                g = (BODY - 1) * SLOTS + s
                message(g, s)
                if g + 2 < NG:
                    window_rows(g + 2, (s + 2) % SLOTS, 0)
                    window_rows(g + 2, (s + 2) % SLOTS, 1)
            act.wait_ge(out0_ready, 1)
            for c, (d0, nd) in enumerate(CHUNKS):
                if c >= 2:
                    act.wait_ge(out0_turned, c - 1)
                nc.scalar.activation(halves_sb[c % 2][:, 0:nd], ps[c][:, 0:nd], ACT.Copy).then_inc(out0_copied, 1)
            def high_half(k):
                c, q, j0, nj = SPLITS[k]
                nd = CHUNKS[c][1]
                act.wait_ge(adj_loaded[STAGE[k]], 32 * STAGE[:k + 1].count(STAGE[k]))
                if (c, q) in streamed_of and streamed_of[c, q] >= RING:
                    v = streamed_of[c, q]
                    act.wait_ge(unit_stored[v % RING], 32 * (v // RING))
                    act.wait_ge(unit_used, v + 1)
                if k in TAKEN:
                    act.wait_ge(stage_free, max(m for m in range(k) if STAGE[m] == TAKEN.index(k)) + 1)
                nc.scalar.activation(split_out(c, q)[:, :, 0, :],
                                     stage[STAGE[k]][:, 0:nj * nd].rearrange("p (j d) -> p j d", d=nd),
                                     ACT.Copy, scale=A_HI).then_inc(adj_hi_ready, 1)

            def store_unit(k):
                if SPLITS[k][:2] in streamed_of:
                    v = streamed_of[SPLITS[k][:2]]
                    act.wait_ge(adj_split, k + 1)
                    for p0, p1 in PARTS:
                        nc.scalar.dma_start(split_d[v, p0:p1],
                                            ring[v % RING][p0:p1].rearrange("p j h d -> p (j h d)")
                                            ).then_inc(unit_stored[v % RING], 16)

            high_half(0)
            high_half(1)
            act.wait_ge(h1_ready, 1)
            nc.scalar.activation(hh[0][0][:, :, 0:C], norm_c, ACT.Copy, scale=H_UP).then_inc(hi_ready, 1)
            act.wait_ge(hh_ready, NC)
            act.sem_inc(bank_free, NC)
            store_unit(0)

            def new_values(i, r0, c):
                d0, nd = CHUNKS[c]
                kk = r0 * NC + c
                k = i * (2 * NC) + kk
                b = kk % 2
                w = nd // P * C
                act.wait_ge(product_ready, k + 1)
                nc.scalar.activation(halves_sb[b][:, 0:nd], ps[ACC[c]][:, 0:nd], ACT.Copy,
                                     scale=UNSCALE).then_inc(bank_free, 1)
                act.wait_ge(turned, k + 1)
                nc.scalar.activation(square[:, 0:w], ps[TURN[c]][0:P, 0:w], ACT.Square).then_inc(squared, 1)
                act.wait_ge(eps_ready, k + 1)
                nc.scalar.activation(n_tanh[b][:, 0:nd // P], n_eps[b][:, 0:nd // P], ACT.Tanh).then_inc(tanh_ready, 1)
                act.wait_ge(new_ready, k + 1)
                nc.scalar.activation(hh[1 - r0 % 2][0][:, d0 // P:(d0 + nd) // P, 0:C],
                                     h_new[:, 0:w].rearrange("p (j c) -> p j c", c=C), ACT.Copy,
                                     scale=H_UP).then_inc(hi_ready, 1)

            for k in range(2, len(SPLITS)):
                high_half(k)
                store_unit(k - 1)
                if k + 1 == len(SPLITS) or SPLITS[k + 1][0] > SPLITS[k][0] > 0:
                    new_values(0, 0, SPLITS[k][0] - 1)
            new_values(0, 0, NC - 1)
            for c in range(NC):
                new_values(0, 1, c)
            with nc.scalar.Fori(0, LAYERS // 2 - 1) as i:
                for r0 in (2, 3):
                    for c in range(NC):
                        new_values(i, r0, c)

        @block.vector
        def _(dve):
            done = [0]

            def link(ins):
                done[0] += 1
                ins.then_inc(dve_step, 1)
                dve.wait_ge(dve_step, done[0])

            def rsqrt(did, y, t, v):
                yi = y.bitcast(I32)
                did(nc.vector.tensor_scalar(yi, v.bitcast(I32), 1, None, ALU.logical_shift_right))
                did(nc.vector.tensor_scalar(yi, yi, -1.0, RSQRT_MAGIC, ALU.mult, ALU.add))
                for _ in range(3):
                    did(nc.vector.scalar_tensor_tensor(out=t, in0=y, scalar=-0.5, in1=y, op0=ALU.mult, op1=ALU.mult))
                    did(nc.vector.tensor_tensor(t, t, v, ALU.mult))
                    did(nc.vector.scalar_tensor_tensor(out=y, in0=t, scalar=1.5, in1=y, op0=ALU.add, op1=ALU.mult))

            def layernorm_relu(x, out, sq):
                mean, var, neg, rstd = (s[:, :] for s in stat)
                wide = (lambda v: v.unsqueeze(2).to_broadcast([P, NJ, C]))
                link(nc.vector.tensor_reduce(out=mean, in_=x, axis=AX.X, op=ALU.add))
                link(nc.vector.tensor_scalar(neg, mean, -1.0 / C, None, ALU.mult))
                link(nc.vector.tensor_tensor(out, x, wide(neg), ALU.add))
                link(nc.vector.tensor_tensor(sq, out, out, ALU.mult))
                link(nc.vector.tensor_reduce(out=var, in_=sq, axis=AX.X, op=ALU.add))
                link(nc.vector.tensor_scalar(neg, var, 1.0 / C, LN_EPS, ALU.mult, ALU.add))
                rsqrt(link, rstd, mean, neg)
                link(nc.vector.tensor_tensor(sq, out, wide(rstd), ALU.mult))
                return nc.vector.tensor_scalar(out, sq, 0.0, None, ALU.max)

            dve.sem_inc(keyrow_free, SLOTS)
            dve.sem_inc(onehot_ready, 1)
            nc.vector.memset(zeros, 0.0).then_inc(zeros_ready, 1)
            nc.vector.memset(zeros16, 0.0).then_inc(zeros_ready, 1)
            dve.wait_ge(x_loaded, 16)
            layernorm_relu(z_acc[:], norm_c, norm_s).then_inc(h0_ready, 1)
            dve.wait_ge(iotas_ready, 4)
            link(nc.vector.tensor_scalar(ident, iota_sq, 0.0, None, ALU.is_equal))
            nc.vector.memset(ones, 1.0)
            nc.vector.memset(before[:, 0:WIDE - 1, :], 1.0)
            nc.vector.tensor_scalar(before[:, WIDE - 1, :], iota_sq, 0.0, None, ALU.is_lt)
            link(nc.vector.tensor_copy(spare_f, spare_i))
            nc.vector.tensor_scalar(row_f, spare_f, -float(N * N), None, ALU.add)
            nc.vector.tensor_scalar(fold_b, iota_fold, -float(C), None, ALU.is_equal)
            link(nc.vector.tensor_scalar(fold[:], iota_fold, 0.0, None, ALU.is_equal))
            link(nc.vector.tensor_tensor(fold[:], fold[:], fold_b, ALU.add))
            dve.sem_inc(ident_ready, 1)
            dve.wait_ge(edges_loaded, 48)
            nc.vector.tensor_copy(dst_row[0:TROWS], dst_row_i[0:TROWS])
            link(nc.vector.tensor_copy(src_row[0:TROWS], src_row_i[0:TROWS]))
            link(nc.vector.scalar_tensor_tensor(
                out=key_row[0:TROWS].rearrange("q a p -> q (a p)"),
                in0=src_row[0:TROWS].rearrange("q a p -> q (a p)"), scalar=float(N),
                in1=dst_row[0:TROWS].rearrange("q a p -> q (a p)"), op0=ALU.mult, op1=ALU.add))
            dve.sem_inc(key_ready, 1)
            for n, column in enumerate((src_f, dst_f, w_up)):
                for half, (a0, a1) in enumerate(((0, 6), (6, G))):
                    dve.wait_ge(rows_turned, 2 * n + half + 1)
                    nc.vector.tensor_copy(column[:, a0 * TROWS:a1 * TROWS],
                                          ps[2 * (n % 2) + half][0:P, 0:(a1 - a0) * TROWS]
                                          ).then_inc(columns_copied, 1)
            dve.wait_ge(columns_copied, 6)
            link(nc.vector.scalar_tensor_tensor(out=key_f, in0=src_f, scalar=float(N), in1=dst_f,
                                                op0=ALU.mult, op1=ALU.add))
            dve.sem_inc(columns_ready, 1)
            dve.wait_ge(bn_loaded, 64)
            link(nc.vector.tensor_scalar(bias, bn[:, 3, :], BN_EPS, None, ALU.add))
            rsqrt(link, inv, bn[:, 3, :], bias)
            link(nc.vector.tensor_tensor(inv, inv, bn[:, 0, :], ALU.mult))
            link(nc.vector.tensor_tensor(bias, inv, bn[:, 2, :], ALU.mult))
            link(nc.vector.tensor_tensor(bias, bn[:, 1, :], bias, ALU.subtract))
            dve.wait_ge(w_turned, 1)
            link(nc.vector.tensor_copy(w_t[0:C, :], ps[3][0:C, 0:2 * C]))
            link(nc.vector.tensor_tensor(w_t[0:C, 0:C], w_t[0:C, 0:C], w_t[0:C, C:2 * C], ALU.subtract))
            nc.vector.tensor_tensor(w_fold[0:C, 0:C], w_t[0:C, 0:C], inv[0:C], ALU.mult).then_inc(w_folded, 1)
            nc.vector.tensor_tensor(w_fold[0:C, C:2 * C], w_t[0:C, C:2 * C], inv[0:C], ALU.mult).then_inc(w_folded, 1)
            for c, (d0, nd) in enumerate(CHUNKS):
                dve.wait_ge(h0_turned, c + 1)
                nc.vector.tensor_copy(h0t[0:C, d0:d0 + nd], ps[4 + c % 2][0:C, 0:nd]).then_inc(h0t_copied, 1)
            for c, (d0, nd) in enumerate(CHUNKS):
                dve.wait_ge(pq_made, c + 1)
                nj = nd // P
                got = ps[6 + c % 2][0:P, 0:nj * 2 * C].rearrange("p (j c) -> p j c", c=2 * C)
                nc.vector.tensor_tensor(pq[:, d0 // P:d0 // P + nj, 0:C], got[:, :, 0:C],
                                        bias.unsqueeze(1).to_broadcast([P, nj, C]), ALU.add)
                link(nc.vector.tensor_copy(pq[:, d0 // P:d0 // P + nj, C:2 * C], got[:, :, C:2 * C]))
                dve.sem_inc(pq_copied, 1)
            link(nc.vector.tensor_scalar(q16[:, :, 0:C], pq[:, :, C:2 * C], Q_UP, None, ALU.mult))
            link(nc.vector.scalar_tensor_tensor(out=q16[:, :, C:2 * C], in0=pq[:, :, C:2 * C], scalar=Q_UP,
                                                in1=q16[:, :, 0:C], op0=ALU.mult, op1=ALU.subtract))
            dve.sem_inc(pq_ready, 1)
            link(nc.vector.tensor_scalar(w_up, w_up, W_UP, None, ALU.mult))
            link(nc.vector.tensor_copy(w16[:, :, 0], w_up))
            link(nc.vector.tensor_tensor(w16[:, :, 1], w_up, w16[:, :, 0], ALU.subtract))
            link(nc.vector.tensor_scalar(to_spare, key_f, -1.0, spare_f, ALU.mult, ALU.add))
            for n in range(1, WIDE):
                own = to_spare.rearrange("p (g k) -> p g k", k=G)[:, :, n:G:WIDE]
                last = nc.vector.tensor_scalar(own, own, float(n * P), None, ALU.add)
            link(last)
            dve.wait_ge(firsts_spread, 1)
            link(nc.vector.tensor_scalar(first_node, ps[4][0:P, 0:NG], float(N - WINDOW), None, ALU.min))
            nc.vector.tensor_copy(first_i, first_node)
            nc.vector.tensor_scalar(window_node, first_node, row_f, None, ALU.add)
            grouped = (lambda v: v.rearrange("p (g k) -> p g k", k=G))
            link(nc.vector.tensor_tensor(grouped(cols), grouped(dst_f),
                                         first_node.unsqueeze(2).to_broadcast([P, NG, G]), ALU.subtract))
            link(nc.vector.tensor_scalar(in_window, cols, 0.0, None, ALU.is_ge))
            link(nc.vector.scalar_tensor_tensor(out=in_window, in0=cols, scalar=float(WINDOW), in1=in_window,
                                                op0=ALU.is_lt, op1=ALU.mult))
            link(nc.vector.tensor_scalar(cols, dst_f, -1.0, float(N), ALU.mult, ALU.add))
            link(nc.vector.tensor_tensor(cols, cols, in_window, ALU.mult))
            link(nc.vector.tensor_tensor(q_index, cols, dst_f, ALU.add))
            link(nc.vector.tensor_reduce(out=inside, in_=in_window, axis=AX.X, op=ALU.add))
            dve.sem_inc(inside_ready, 1)
            dve.wait_ge(inside_summed, 1)
            link(nc.vector.tensor_scalar(outside, ps[5][0:P, 0:1], -1.0, float(E), ALU.mult, ALU.add))
            link(nc.vector.tensor_reduce(out=last_first, in_=first_node[:, 0:SLOTS], axis=AX.X, op=ALU.max))
            link(nc.vector.tensor_scalar(last_first, last_first, -float(CHUNK - WINDOW), 0.0, ALU.add, ALU.max))
            link(nc.vector.tensor_tensor(beyond, last_first, outside, ALU.add))
            dve.sem_inc(windows_ready, 1)

            base0 = done[0]

            def counted(step0, steps):
                step = [0]

                def did(ins):
                    step[0] += 1
                    assert step[0] <= steps
                    ins.then_inc(dve_step, 1)
                    dve.wait_ge(dve_step, step0 + step[0])
                return did

            def prep_columns(g, slot_turn, s, step0, used_before=True):
                did = counted(step0, 1)
                own = bass.ds(g * G, G)
                dve.wait_ge(bundles_begun, g * NB + 1)
                if used_before:
                    dve.wait_ge(onehot_ready, (g - 2) * G + 1)
                nc.vector.tensor_copy(w16_c[s], w16[:, own, :])
                nc.vector.tensor_copy(src_x[s], src_f[:, own])
                nc.vector.tensor_copy(src_c[s], src_f[:, own])
                nc.vector.tensor_copy(node_c, window_node[:, bass.ds(g, 1)])
                did(nc.vector.tensor_copy(key_c, key_f[:, own]))
                dve.wait_ge(keyrow_loaded[s], slot_turn * 80 + 80)

            def prep_repeats(s, tiles):
                at = 0
                for bundle in BUNDLES:
                    for n, k in enumerate(bundle):
                        w = (n + 1) * P
                        if k in tiles:
                            nc.vector.scalar_tensor_tensor(
                                out=repeat[:, at:at + w],
                                in0=keyrow[s][:, bundle[0]:k + 1, :].rearrange("p a b -> p (a b)"),
                                scalar=key_c[:, k:k + 1],
                                in1=before[:, WIDE - 1 - n:WIDE, :].rearrange("p a b -> p (a b)"),
                                op0=ALU.is_equal, op1=ALU.mult, accum_out=count[s][:, k:k + 1])
                        at += w

            def prep_window(s, step0):
                counted(step0 + 1, 1)(nc.vector.tensor_scalar(pick_dst[s], dstrow[s], node_c, None, ALU.is_equal))
                dve.sem_inc(keyrow_free, 1)
                dve.sem_inc(repeat_ready, 1)

            def prep_scatter(g, s, step0):
                did = counted(step0 + 2, 4)
                own = bass.ds(g * G, G)
                did(nc.vector.scalar_tensor_tensor(out=shift, in0=count[s], scalar=1.0, in1=to_spare[:, own],
                                                   op0=ALU.min, op1=ALU.mult))
                did(nc.vector.tensor_tensor(adj_x[s], shift, key_f[:, own], ALU.add))
                dve.wait_ge(repeat_out, g + 1)
                did(nc.vector.tensor_reduce(out=shift, in_=later[s].rearrange("p (k h) -> p k h", h=2), axis=AX.X, op=ALU.add))
                did(nc.vector.tensor_tensor(w_sum[s], w_up[:, own], shift, ALU.add))
                dve.sem_inc(prep_ready, 1)

            def onehot_rows(g, s, tiles):
                for k in tiles:
                    dve.wait_ge(onehot_free, g * G + (k + 1))
                    nc.vector.tensor_scalar(onehot[(s * G + k) % OH], iota16, src_c[s][:, k:k + 1], None,
                                            ALU.is_equal).then_inc(onehot_ready, 1)

            def use(g, slot_turn, s, ahead):
                dve.wait_ge(gathered[s], slot_turn * (16 * G) + 16 * G)
                dve.wait_ge(q_ready, g + 1)
                dve.wait_ge(window_out, g * 2 + (2 + 2 * SLOTS))
                nc.vector.tensor_tensor(msg[s], p_g[s], msg[s], ALU.add).then_inc(pre_ready, 1)
                onehot_rows(g, s, (0,))
                if ahead:
                    g2, slot_turn2, s2, step2 = ahead
                    prep_columns(*ahead)
                dve.wait_ge(msg_hi_ready, g + 1)
                nc.vector.tensor_tensor(msg16[s][:, :, C:2 * C], msg[s], msg16[s][:, :, 0:C],
                                        ALU.subtract).then_inc(msg_ready, 1)
                for k in range(1, G):
                    onehot_rows(g, s, (k,))
                    if ahead and k < 6:
                        prep_repeats(s2, ((0, 1), (2, 3), (4, 5), (6, 7, 8), (9, 10))[k - 1])
                    if ahead and k == 6:
                        prep_window(s2, step2)
                if ahead:
                    prep_scatter(g2, s2, step2)

            S = 6
            for g in range(2):
                prep_columns(g, 0, g, base0 + S * g, used_before=False)
                prep_repeats(g, range(G))
                prep_window(g, base0 + S * g)
                prep_scatter(g, g, base0 + S * g)
            with nc.vector.Fori(0, BODY - 1) as i:
                for s in range(SLOTS):
                    use(i * SLOTS + s, i, s, (i * SLOTS + (s + 2), i + (s + 2) // SLOTS, (s + 2) % SLOTS,
                                              i * (S * SLOTS) + (base0 + S * (s + 2))))
            for s in range(SLOTS):
                g = (BODY - 1) * SLOTS + s
                use(g, g // SLOTS, s, (g + 2, (g + 2) // SLOTS, (s + 2) % SLOTS, base0 + S * (g + 2))
                    if g + 2 < NG else None)
            done[0] = base0 + S * NG

            for c, (d0, nd) in enumerate(CHUNKS):
                nj = nd // P
                v = z_acc[:, d0 // P:d0 // P + nj, :]
                dve.wait_ge(out0_turned, c + 1)
                nc.vector.tensor_tensor(v, v, ps[c][0:P, 0:nj * C].rearrange("p (j c) -> p j c", c=C),
                                        ALU.add).then_inc(out0_added, 1)
            dve.wait_ge(out0_added, NC)
            link(layernorm_relu(z_acc[:], norm_c, norm_s))
            dve.sem_inc(h1_ready, 1)
            dve.wait_ge(mix_loaded, 16)
            link(nc.vector.scalar_tensor_tensor(out=z_acc[:], in0=norm_c, scalar=mix[:, 0:1], in1=z_acc[:],
                                                op0=ALU.mult, op1=ALU.add))
            dve.wait_ge(hi_ready, 1)
            link(nc.vector.scalar_tensor_tensor(out=hh[0][0][:, :, C:2 * C], in0=norm_c, scalar=H_UP,
                                                in1=hh[0][0][:, :, 0:C], op0=ALU.mult, op1=ALU.subtract))
            link(nc.vector.tensor_scalar(hh[0][1], hh[0][0], A_HI, None, ALU.mult))
            dve.sem_inc(hh_ready, NC)
            def low_halves(c):
                for k, (cc, q, j0, nj) in enumerate(SPLITS):
                    if cc != c:
                        continue
                    nd = CHUNKS[c][1]
                    dve.wait_ge(adj_hi_ready, k + 1)
                    o = split_out(c, q)
                    nc.vector.scalar_tensor_tensor(out=o[:, :, 1, :], in0=o[:, :, 0, :], scalar=-1.0 / A_HI,
                                                   in1=stage[STAGE[k]][:, 0:nj * nd].rearrange("p (j d) -> p j d", d=nd),
                                                   op0=ALU.mult, op1=ALU.add).then_inc(adj_split, 1)
                    dve.wait_ge(adj_split, k + 1)
                    dve.sem_inc(stage_free, 1)

            base1 = done[0]
            STEPS = 17

            def new_values(i, r0, c):
                d0, nd = CHUNKS[c]
                kk = r0 * NC + c
                k = i * (2 * NC) + kk
                b = kk % 2
                nj = nd // P
                w = nj * C
                layer = i * 2 + (r0 + 1)
                step = [0]

                def did(ins):
                    step[0] += 1
                    ins.then_inc(dve_step, 1)
                    dve.wait_ge(dve_step, i * (2 * NC * STEPS) + (base1 + kk * STEPS + step[0]))

                new = h_new[:, 0:w].rearrange("p (j c) -> p j c", c=C)
                n_s, n_e, n_t, f = (v[b][:, 0:nj] for v in (n_sq, n_eps, n_tanh, factor))
                dve.wait_ge(squared, k + 1)
                did(nc.vector.tensor_reduce(out=n_s, in_=square[:, 0:w].rearrange("p (j c) -> p j c", c=C),
                                            axis=AX.X, op=ALU.add))
                rsqrt(did, f, n_e, n_s)
                did(nc.vector.tensor_tensor(n_t, f, n_s, ALU.mult))
                nc.vector.tensor_scalar(n_e, n_t, NORM_EPS, None, ALU.add).then_inc(eps_ready, 1)
                dve.wait_ge(eps_ready, k + 1)
                did(nc.vector.reciprocal(n_s, n_e))
                dve.wait_ge(tanh_ready, k + 1)
                did(nc.vector.tensor_tensor(f, n_t, n_s, ALU.mult))
                nc.vector.tensor_tensor(new, ps[TURN[c]][0:P, 0:w].rearrange("p (j c) -> p j c", c=C),
                                        f.unsqueeze(2).to_broadcast([P, nj, C]), ALU.mult).then_inc(new_ready, 1)
                dve.wait_ge(new_ready, k + 1)
                zc = z_acc[:, d0 // P:d0 // P + nj, :]
                nc.vector.scalar_tensor_tensor(out=zc, in0=new, scalar=mix[:, bass.ds(layer, 1)], in1=zc,
                                               op0=ALU.mult, op1=ALU.add)
                dve.wait_ge(hi_ready, k + 2)
                own = hh[1 - r0 % 2][0][:, d0 // P:d0 // P + nj, :]
                did(nc.vector.scalar_tensor_tensor(out=own[:, :, C:2 * C], in0=new, scalar=H_UP,
                                                   in1=own[:, :, 0:C], op0=ALU.mult, op1=ALU.subtract))
                did(nc.vector.tensor_scalar(hh[1 - r0 % 2][1][:, d0 // P:d0 // P + nj, :], own, A_HI, None, ALU.mult))
                dve.sem_inc(hh_ready, 1)
                assert step[0] == STEPS

            low_halves(0)
            for c in range(1, NC):
                low_halves(c)
                new_values(0, 0, c - 1)
            new_values(0, 0, NC - 1)
            for c in range(NC):
                new_values(0, 1, c)
            with nc.vector.Fori(0, LAYERS // 2 - 1) as i:
                for r0 in (2, 3):
                    for c in range(NC):
                        new_values(i, r0, c)

        @block.tensor
        def _(pe):
            pe.wait_ge(ident_ready, 1)
            pe.wait_ge(key_ready, 1)
            for n, row in enumerate((src_row, dst_row, w_row)):
                for half, (a0, a1) in enumerate(((0, 6), (6, G))):
                    if n == 2:
                        pe.wait_ge(columns_copied, half + 1)
                    for a in range(a0, a1):
                        last = nc.tensor.transpose(ps[2 * (n % 2) + half][0:P, (a - a0) * TROWS:(a - a0 + 1) * TROWS],
                                                   row[0:TROWS, a, :], ident[0:TROWS, 0:TROWS])
                    last.then_inc(rows_turned, 1)
            pe.wait_ge(columns_ready, 1)
            pe.wait_ge(w_loaded, 16)
            for h in range(2):
                last = nc.tensor.transpose(ps[3][0:C, h * C:(h + 1) * C], w_nat[0:C, h * C:(h + 1) * C],
                                           ident[0:C, 0:C])
            last.then_inc(w_turned, 1)
            pe.wait_ge(h0_ready, 1)
            for c, (d0, nd) in enumerate(CHUNKS):
                if c >= 2:
                    pe.wait_ge(h0t_copied, c - 1)
                for u in range(nd // P):
                    last = nc.tensor.transpose(ps[4 + c % 2][0:C, u * P:(u + 1) * P], norm_c[:, d0 // P + u, :], ident)
                last.then_inc(h0_turned, 1)
            pe.wait_ge(w_folded, 2)
            pe.wait_ge(h0t_copied, NC)
            for c, (d0, nd) in enumerate(CHUNKS):
                if c >= 2:
                    pe.wait_ge(pq_copied, c - 1)
                for u in range(nd // P):
                    last = nc.tensor.matmul(ps[6 + c % 2][0:P, u * 2 * C:(u + 1) * 2 * C],
                                            h0t[0:C, d0 + u * P:d0 + (u + 1) * P], w_fold[0:C, :],
                                            start=True, stop=True)
                last.then_inc(pq_made, 1)
            pe.wait_ge(pq_ready, 1)
            nc.tensor.matmul(ps[4][0:P, 0:NG], ones[0:1, :], dst_f[0:1, 0:T:G], start=True,
                             stop=True).then_inc(firsts_spread, 1)
            pe.wait_ge(inside_ready, 1)
            nc.tensor.matmul(ps[5][0:P, 0:1], ones, inside, start=True, stop=True).then_inc(inside_summed, 1)
            pe.wait_ge(windows_ready, 1)

            pe.wait_ge(zeros_ready, 2)
            pe.wait_ge(pq_ready, 1)
            for c, (d0, nd) in enumerate(CHUNKS):
                nc.tensor.matmul(ps[c][:, 0:nd], zeros16[:, 0:128], zeros16[:, 128:128 + nd], start=True, stop=False)
            pe.sem_inc(onehot_free, OH)

            def sum_repeats(g, s):
                pe.wait_ge(repeat_ready, g + 1)
                at = 0
                for bundle in BUNDLES:
                    starts = []
                    for n in range(len(bundle)):
                        starts.append(at)
                        at += (n + 1) * P
                    for m, k in enumerate(bundle):
                        for n in range(m, len(bundle)):
                            nc.tensor.matmul(
                                ps[7][0:P, REP_AT + 2 * k:REP_AT + 2 * k + 2],
                                repeat[:, starts[n] + m * P:starts[n] + (m + 1) * P],
                                w16_c[s][:, bundle[n], :], start=(n == m), stop=(n == len(bundle) - 1))

            def window_rows(g, s, piece):
                k0, k1 = PIECES[piece]
                for k in range(k0, k1):
                    for h in range(2):
                        last = nc.tensor.matmul(ps[7][0:P, (k - k0) * C:(k - k0 + 1) * C], pick_dst[s][0:WINDOW, k, :],
                                                q_window[s][0:WINDOW, h * C:(h + 1) * C], start=(h == 0), stop=(h == 1))
                last.then_inc(window_made, 1)

            def second_piece(g, s):
                pe.wait_ge(window_out, g * 2 + (1 + 2 * SLOTS))
                window_rows(g, s, 1)

            def add_messages(g, s, tiles):
                pe.wait_ge(msg_ready, g + 1)
                for k in tiles:
                    pe.wait_ge(onehot_ready, g * G + (k + 2))
                    for c, (d0, nd) in enumerate(CHUNKS):
                        last = nc.tensor.matmul(ps[c][:, 0:nd], msg16[s][:, k, :],
                                                onehot[(s * G + k) % OH][:, d0:d0 + nd], start=False, stop=False)
                    last.then_inc(onehot_free, 1)

            def group(g, s, ahead):
                n = (s + 2) % SLOTS
                add_messages(g, s, range(0, 7))
                if ahead:
                    pe.wait_ge(window_out, g * 2 + (4 + 2 * SLOTS))
                    sum_repeats(g + 2, n)
                    window_rows(g + 2, n, 0)
                add_messages(g, s, range(7, 9))
                if ahead:
                    second_piece(g + 2, n)
                add_messages(g, s, range(9, G))

            for g in range(2):
                if g:
                    pe.wait_ge(window_out, 2 + 2 * SLOTS)
                sum_repeats(g, g)
                window_rows(g, g, 0)
                second_piece(g, g)
            with nc.tensor.Fori(0, BODY - 1) as i:
                for s in range(SLOTS):
                    group(i * SLOTS + s, s, True)
            for s in range(SLOTS):
                g = (BODY - 1) * SLOTS + s
                group(g, s, g + 2 < NG)
            for c, (d0, nd) in enumerate(CHUNKS):
                last = nc.tensor.matmul(ps[c][:, 0:nd], zeros16[:, 0:128], zeros16[:, 128:128 + nd],
                                        start=False, stop=True)
            last.then_inc(out0_ready, 1)
            for c, (d0, nd) in enumerate(CHUNKS):
                pe.wait_ge(out0_copied, c + 1)
                for u in range(nd // P):
                    last = nc.tensor.matmul(ps[c][0:P, u * C:(u + 1) * C], halves_sb[c % 2][:, u * P:(u + 1) * P],
                                            fold[:], start=True, stop=True)
                last.then_inc(out0_turned, 1)

            pe.sem_inc(unit_used, RING)

            def turn(c, k, b):
                pe.wait_ge(bank_free, k + (NC + 1))
                for u in range(CHUNKS[c][1] // P):
                    last = nc.tensor.matmul(ps[TURN[c]][0:P, u * C:(u + 1) * C], halves_sb[b][:, u * P:(u + 1) * P],
                                            fold[:], start=True, stop=True)
                last.then_inc(turned, 1)

            def multiply(i, r0):
                for c, (d0, nd) in enumerate(CHUNKS):
                    kk = r0 * NC + c
                    k = i * (2 * NC) + kk
                    pe.wait_ge(bank_free, k + (NC + 1 - (3 if 3 <= c < NC - 1 else 4 if c < 3 else NC)))
                    for j in range(NJ):
                        if c == 0 and j % BPC == 0:
                            pe.wait_ge(hh_ready, i * (2 * NC) + (r0 * NC + j // BPC + 1))
                        q, jj = (j // UJ, j % UJ) if c < NC - 1 else (j // 20, j % 20)
                        if r0 == 0 and jj == 0:
                            pe.wait_ge(adj_split, 1 + [u[:2] for u in SPLITS].index((c, q)))
                        if c == NC - 1 or (c, q) in resident_of or r0 == 0:
                            a = split_out(c, q)[:, jj]
                        else:
                            v = streamed_of[c, q]
                            a = ring[v % RING][:, jj]
                            if jj == 0:
                                turns = STREAMED // RING
                                pe.wait_ge(streamed[v % RING],
                                           i * (2 * turns * 32) + 32 * ((r0 - 1) * turns + v // RING + 1))
                        for part in range(2):
                            last = nc.tensor.matmul(ps[ACC[c]][:, 0:nd], hh[r0 % 2][part][:, j, :], a[:, part, :],
                                                    start=(j == 0 and part == 0), stop=(j == NJ - 1 and part == 1))
                        if (c, q) in streamed_of and jj == UJ - 1:
                            last.then_inc(unit_used, 1)
                        if c > 0 and j == 12:
                            turn(c - 1, k - 1, (kk - 1) % 2)
                        if c == 0 and j == 9 and r0 > 0:
                            turn(NC - 1, k - 1, (kk - 1) % 2)
                    last.then_inc(product_ready, 1)

            multiply(0, 0)
            multiply(0, 1)
            with nc.tensor.Fori(0, LAYERS // 2 - 1) as i:
                multiply(i, 2)
                multiply(i, 3)
            turn(NC - 1, LAYERS * NC - 1, (LAYERS * NC - 1) % 2)


PARTS = ((0, 112), (112, P))
REP_AT = 400
ACC = [0, 1, 2, 0, 1, 2, 3]
TURN = [4, 5, 6, 4, 5, 6, 7]


_INS = ['x', 'src', 'dst', 'edge_weight', 'L0_gnn_W', 'L0_gnn_bn_gamma', 'L0_gnn_bn_beta', 'L0_gnn_bn_mean',
        'L0_gnn_bn_var', 'L1_gnn_manifold_weights']


def kernel(**inputs):
    import numpy as _np
    import concourse.bacc as _bacc
    from concourse import mybir as _mybir
    from concourse.bass_utils import run_bass_kernel_spmd as _run

    nc = _bacc.Bacc("TRN2", target_bir_lowering=False, num_devices=1)
    arrays, args = {}, []
    for name in _INS:
        a = _np.ascontiguousarray(inputs[name])
        arrays[f"in_{name}_dram"] = a
        args.append(nc.dram_tensor(f"in_{name}_dram", a.shape, _mybir.dt.from_np(a.dtype), kind="ExternalInput").ap())
    args.append(nc.dram_tensor("out_0_dram", (N, C), _mybir.dt.float32, kind="ExternalOutput").ap())
    gnn_kernel(nc, *args)
    r = _run(nc, [arrays], core_ids=[0])
    return r.results[0]["out_0_dram"]
```
